# Optimizing a Trainium2 kernel written in Bass

```python
import numpy as np
import jax
import jax.numpy as jnp

def _softmax(x, axis=-1):
    return jax.nn.softmax(x, axis=axis)

def _gelu(x):
    return jax.nn.gelu(x, approximate=True)

def _silu(x):
    return jax.nn.silu(x)

def _sigmoid(x):
    return jax.nn.sigmoid(x)

def _layernorm(x, axis=-1, eps=1e-05):
    m = jnp.mean(x, axis=axis, keepdims=True)
    v = jnp.var(x, axis=axis, keepdims=True)
    return (x - m) / jnp.sqrt(v + eps)

def _scatter_add(tgt, idx, src, axis=0):
    return tgt.at[idx].add(src)

def _segment_sum(src, seg, n):
    return jax.ops.segment_sum(src, seg, n)
kernel_name = 'mk_adaln_attn_ffn_d1_seqx_r8_a2a8ef'

def setup_inputs(seed: int=0):
    np.random.seed(seed)
    _w = jnp.asarray

    def _rec_inputs():
        import jax
        import jax.numpy as jnp
        _rk = jax.random.key(seed)
        x = -7.109e-05 + 0.9999 * jax.random.normal(jax.random.fold_in(_rk, 1), (64, 32, 512), jnp.float32)
        _lenS = 32 - jax.random.randint(jax.random.fold_in(_rk, 7), (64,), 0, max(1, 32 // 4) + 1, jnp.int32)
        _lenS2 = 32 - jax.random.randint(jax.random.fold_in(_rk, 8), (64,), 0, max(1, 32 // 4) + 1, jnp.int32)
        itok_B_0_15 = jax.random.randint(jax.random.fold_in(_rk, 11), (64,), 0, 16, jnp.int32)
        itok_B_2_6 = jax.random.randint(jax.random.fold_in(_rk, 12), (64,), 2, 7, jnp.int32)
        return (x, itok_B_0_15, itok_B_2_6)
    x, itok_B_0_15, itok_B_2_6 = _rec_inputs()

    def _L0_cond_setup():
        import jax, jax.numpy as jnp
        import numpy as np
        NUM_CONDITIONS = 16
        IN_CH = 32
        OUT_CH = 32
        B = 64
        T = 512
        key = jax.random.key(seed)
        k_x, k_w, k_c = jax.random.split(key, 3)
        x = jax.random.normal(k_x, (B, IN_CH, T), dtype=jnp.float32)
        bound = float(np.sqrt(6.0 / IN_CH))
        weights = jax.random.uniform(k_w, (NUM_CONDITIONS, IN_CH, OUT_CH), dtype=jnp.float32, minval=-bound, maxval=bound)
        condition = jax.random.randint(k_c, (B,), 0, NUM_CONDITIONS, dtype=jnp.int64)
        return {'x': x, 'weights': weights, 'condition': condition}
    _L0_cond_all = _L0_cond_setup()
    _L0_cond_in = {k: v for k, v in _L0_cond_all.items() if k in ('weights',)}
    del _L0_cond_all

    def _L0_attn_setup():
        import jax, jax.numpy as jnp
        import numpy as np
        BATCH, SEQ, HIDDEN = (2, 512, 512)
        HEADS, HEAD_DIM, BLOCK = (32, 128, 32)
        LAYER_IDX, N_LAYERS = (1, 32)
        EPS = 1e-05

        def _decays():
            base = 1.0 / 2.0 ** (8.0 / HEADS)
            exponent = jnp.arange(HEADS, dtype=jnp.float32) + 1.0
            factor = 1.0 - LAYER_IDX / (N_LAYERS - 1 + 1e-05) + 1e-05
            slope = (base ** exponent * factor)[:, None, None]
            r = jnp.arange(BLOCK, dtype=jnp.float32) + 1.0
            q_decay = jnp.exp(-slope * r[:, None])
            k_decay = jnp.exp(-slope * (BLOCK - r)[:, None])
            diff = r[:, None] - r[None, :]
            diag = slope[None] * diff[None, None]
            diag = jnp.where(diag >= 0, -diag, -jnp.inf)
            diag_decay = jnp.exp(diag)
            block_decay = jnp.exp(-slope * BLOCK)
            return (q_decay, k_decay, diag_decay, block_decay)
        key = jax.random.key(seed)
        ks = jax.random.split(key, 5)
        s = 0.02
        return {'hidden_states': jax.random.normal(ks[0], (BATCH, SEQ, HIDDEN), jnp.float32), 'qkv_w': jax.random.normal(ks[1], (3 * HEADS * HEAD_DIM, HIDDEN), jnp.float32) * s, 'out_w': jax.random.normal(ks[2], (HIDDEN, HEADS * HEAD_DIM), jnp.float32) * s, 'gate_w': jax.random.normal(ks[3], (HEADS * HEAD_DIM, HIDDEN), jnp.float32) * s, 'norm_w': jnp.ones((HEADS * HEAD_DIM,), jnp.float32)}
    _L0_attn_all = _L0_attn_setup()
    _L0_attn_in = {k: v for k, v in _L0_attn_all.items() if k in ('qkv_w', 'out_w', 'gate_w', 'norm_w')}
    del _L0_attn_all

    def _L0_cond2_setup():
        import jax, jax.numpy as jnp
        import numpy as np
        B, N, H, F = (4, 64, 512, 1376)
        L, R, RANK = (1, 16, 16)
        SCALE = 0.5
        key = jax.random.key(seed)
        ks = jax.random.split(key, 12)
        nrm = lambda k, shape, fan: jax.random.normal(k, shape, jnp.float32) * fan ** (-0.5)
        inp = {'x': jax.random.normal(ks[0], (B, N, H), jnp.float32), 'W_gate': nrm(ks[1], (F, H), H), 'W_up': nrm(ks[2], (F, H), H), 'W_down': nrm(ks[3], (H, F), F), 'A_gate': nrm(ks[4], (L, R, RANK, H), H), 'B_gate': nrm(ks[5], (L, R, F, RANK), RANK), 'A_up': nrm(ks[6], (L, R, RANK, H), H), 'B_up': nrm(ks[7], (L, R, F, RANK), RANK), 'A_down': nrm(ks[8], (L, R, RANK, F), F), 'B_down': nrm(ks[9], (L, R, H, RANK), RANK), 'lora_indices': jax.random.randint(ks[10], (B,), 0, R), 'layer_idx': 0}
        return inp
    _L0_cond2_all = _L0_cond2_setup()
    _L0_cond2_in = {k: v for k, v in _L0_cond2_all.items() if k in ('W_gate', 'W_up', 'W_down', 'A_gate', 'B_gate', 'A_up', 'B_up', 'A_down', 'B_down')}
    del _L0_cond2_all

    def _L0_ffn_setup():
        import jax, jax.numpy as jnp
        import numpy as np

        def binarize_weight(W):
            alpha = jnp.mean(jnp.abs(W), axis=tuple(range(1, W.ndim)), keepdims=True)
            return alpha * jnp.sign(W)
        key = jax.random.key(seed)
        k1, k2, k3 = jax.random.split(key, 3)
        B, S, D_IN, D_OUT = (4, 256, 512, 512)
        x = jax.random.normal(k1, (B, S, D_IN), dtype=jnp.float32)
        weight_real = jax.random.normal(k2, (D_OUT, D_IN), dtype=jnp.float32)
        bias = jax.random.normal(k3, (D_OUT,), dtype=jnp.float32)
        return {'x': x, 'weight_real': weight_real, 'bias': bias}
    _L0_ffn_all = _L0_ffn_setup()
    _L0_ffn_in = {k: v for k, v in _L0_ffn_all.items() if k in ('weight_real', 'bias')}
    del _L0_ffn_all
    return {'x': x, 'itok_B_0_15': itok_B_0_15, 'itok_B_2_6': itok_B_2_6, 'L0_cond_weights': _L0_cond_in['weights'], 'L0_attn_qkv_w': _L0_attn_in['qkv_w'], 'L0_attn_out_w': _L0_attn_in['out_w'], 'L0_attn_gate_w': _L0_attn_in['gate_w'], 'L0_attn_norm_w': _L0_attn_in['norm_w'], 'L0_cond2_W_gate': _L0_cond2_in['W_gate'], 'L0_cond2_W_up': _L0_cond2_in['W_up'], 'L0_cond2_W_down': _L0_cond2_in['W_down'], 'L0_cond2_A_gate': _L0_cond2_in['A_gate'], 'L0_cond2_B_gate': _L0_cond2_in['B_gate'], 'L0_cond2_A_up': _L0_cond2_in['A_up'], 'L0_cond2_B_up': _L0_cond2_in['B_up'], 'L0_cond2_A_down': _L0_cond2_in['A_down'], 'L0_cond2_B_down': _L0_cond2_in['B_down'], 'L0_ffn_weight_real': _L0_ffn_in['weight_real'], 'L0_ffn_bias': _L0_ffn_in['bias']}

def reference(x, itok_B_0_15, itok_B_2_6, L0_cond_weights, L0_attn_qkv_w, L0_attn_out_w, L0_attn_gate_w, L0_attn_norm_w, L0_cond2_W_gate, L0_cond2_W_up, L0_cond2_W_down, L0_cond2_A_gate, L0_cond2_B_gate, L0_cond2_A_up, L0_cond2_B_up, L0_cond2_A_down, L0_cond2_B_down, L0_ffn_weight_real, L0_ffn_bias):
    import jax
    import jax.numpy as jnp

    def _L0_cond_ref(x, weights, condition):
        import jax, jax.numpy as jnp
        import numpy as np
        NUM_CONDITIONS = 16
        IN_CH = 32
        OUT_CH = 32
        B = 64
        T = 512
        W = weights[condition]
        return jnp.einsum('bct,bcd->bdt', x, W)

    def _L0_attn_ref(hidden_states, qkv_w, out_w, gate_w, norm_w):
        import jax, jax.numpy as jnp
        import numpy as np
        BATCH, SEQ, HIDDEN = (2, 512, 512)
        HEADS, HEAD_DIM, BLOCK = (32, 128, 32)
        LAYER_IDX, N_LAYERS = (1, 32)
        EPS = 1e-05

        def _decays():
            base = 1.0 / 2.0 ** (8.0 / HEADS)
            exponent = jnp.arange(HEADS, dtype=jnp.float32) + 1.0
            factor = 1.0 - LAYER_IDX / (N_LAYERS - 1 + 1e-05) + 1e-05
            slope = (base ** exponent * factor)[:, None, None]
            r = jnp.arange(BLOCK, dtype=jnp.float32) + 1.0
            q_decay = jnp.exp(-slope * r[:, None])
            k_decay = jnp.exp(-slope * (BLOCK - r)[:, None])
            diff = r[:, None] - r[None, :]
            diag = slope[None] * diff[None, None]
            diag = jnp.where(diag >= 0, -diag, -jnp.inf)
            diag_decay = jnp.exp(diag)
            block_decay = jnp.exp(-slope * BLOCK)
            return (q_decay, k_decay, diag_decay, block_decay)
        b, s, _ = hidden_states.shape
        h, d, bs = (HEADS, HEAD_DIM, BLOCK)
        nb = s // bs
        q_decay, k_decay, diag_decay, block_decay = _decays()
        qkv = jax.nn.silu(hidden_states @ qkv_w.T)
        qkv = qkv.reshape(b, s, h, 3, d)
        q = jnp.moveaxis(qkv[:, :, :, 0], 2, 1)
        k = jnp.moveaxis(qkv[:, :, :, 1], 2, 1)
        v = jnp.moveaxis(qkv[:, :, :, 2], 2, 1)

        def to_blocks(x):
            return jnp.moveaxis(x.reshape(b, h, nb, bs, d), 2, 0)
        qb, kb, vb = (to_blocks(q), to_blocks(k), to_blocks(v))

        def step(kv, blk):
            cq, ck, cv = blk
            scores = jnp.einsum('bhnd,bhmd->bhnm', cq, ck) * diag_decay
            intra = jnp.einsum('bhnm,bhmd->bhnd', scores, cv)
            inter = jnp.einsum('bhnd,bhde->bhne', cq * q_decay, kv)
            kv_next = kv * block_decay + jnp.einsum('bhnd,bhne->bhde', ck * k_decay, cv)
            return (kv_next, intra + inter)
        kv0 = jnp.zeros((b, h, d, d), hidden_states.dtype)
        _, out_blocks = jax.lax.scan(step, kv0, (qb, kb, vb))
        attn = jnp.moveaxis(out_blocks, 0, 2)
        attn = attn.reshape(b, h, s, d).transpose(0, 2, 1, 3).reshape(b, s, h * d)
        xf = attn.astype(jnp.float32)
        xf = xf * jax.lax.rsqrt(jnp.mean(xf * xf, axis=-1, keepdims=True) + EPS)
        normed = norm_w * xf.astype(attn.dtype)
        gate = jax.nn.sigmoid(hidden_states @ gate_w.T)
        return gate * normed @ out_w.T

    def _L0_cond2_ref(x, W_gate, W_up, W_down, A_gate, B_gate, A_up, B_up, A_down, B_down, lora_indices, layer_idx):
        import jax, jax.numpy as jnp
        import numpy as np
        B, N, H, F = (4, 64, 512, 1376)
        L, R, RANK = (1, 16, 16)
        SCALE = 0.5

        def lora_add(base, inp, A, B):
            Ab = A[layer_idx][lora_indices]
            Bb = B[layer_idx][lora_indices]
            t = jnp.einsum('bri,bni->bnr', Ab, inp)
            return base + jnp.einsum('bor,bnr->bno', Bb, t) * SCALE
        gate = lora_add(jnp.einsum('bnh,fh->bnf', x, W_gate), x, A_gate, B_gate)
        up = lora_add(jnp.einsum('bnh,fh->bnf', x, W_up), x, A_up, B_up)
        act = jax.nn.silu(gate) * up
        down = lora_add(jnp.einsum('bnf,hf->bnh', act, W_down), act, A_down, B_down)
        return down

    def _L0_ffn_ref(x, weight_real, bias):
        import jax, jax.numpy as jnp
        import numpy as np

        def binarize_weight(W):
            alpha = jnp.mean(jnp.abs(W), axis=tuple(range(1, W.ndim)), keepdims=True)
            return alpha * jnp.sign(W)
        W = binarize_weight(weight_real)
        return jnp.einsum('bsi,oi->bso', x, W) + bias
    x = x + _L0_attn_ref(_L0_cond_ref(x, L0_cond_weights, itok_B_0_15), L0_attn_qkv_w, L0_attn_out_w, L0_attn_gate_w, L0_attn_norm_w)
    x = x + _L0_ffn_ref(_L0_cond2_ref(x, L0_cond2_W_gate, L0_cond2_W_up, L0_cond2_W_down, L0_cond2_A_gate, L0_cond2_B_gate, L0_cond2_A_up, L0_cond2_B_up, L0_cond2_A_down, L0_cond2_B_down, itok_B_2_6, 0), L0_ffn_weight_real, L0_ffn_bias)
    return x

_drawn_inputs = setup_inputs


def setup_inputs(seed=0):
    import zlib

    import numpy as np

    out = dict(_drawn_inputs(seed))
    spreads = {'L0_attn_norm_w': (1.0, 0.2)}
    factors = {}
    for name, (base, spread) in spreads.items():
        noise = np.random.default_rng([zlib.crc32(name.encode()), seed]).standard_normal(out[name].shape)
        drawn = base * np.exp(spread * noise) if base else spread * noise
        out[name] = jnp.asarray(drawn.astype(out[name].dtype))
    for name, factor in factors.items():
        out[name] = (out[name] * factor).astype(out[name].dtype)
    return out
```

```python
from contextlib import ExitStack

import numpy as np

import concourse.bass as bass
from concourse import mybir

F32 = mybir.dt.float32
F32R = mybir.dt.float32r
I32 = mybir.dt.int32
U32 = mybir.dt.uint32
ALU = mybir.AluOpType
ACT = mybir.ActivationFunctionType

P = 128
BATCH, SEQ, HID = 64, 32, 512
TOK = BATCH * SEQ
KH = HID // P
NT = 512
NC = TOK // NT
TILES = TOK // P
TPC = NT // P
BPC = NT // SEQ
HEADS, D = 32, 128
CONDS, RANK = 16, 16
RK = CONDS * RANK // P
F = 1376
FC = -(-F // P)
EPS = 1e-5
HD = HEADS * D
UNITS = HEADS * NC
FUNITS = FC * NC
Q, K, G, O = range(4)
FOUT = KH + RK
FW_AT = [0, 512, 1024, 1536, 1792]


def wait(eng, sem, value):
    if not isinstance(value, int) or value > 0:
        eng.wait_ge(sem, value)


def build(nc, x_tok, x_t, cond_idx, lora_idx, consts, cond_w, head_w, v_w, misc, a_w, ffn_w, b_w,
          bdown_w, lin_t, lin_n, bias, out):
    with ExitStack() as ctx:
        def sem(name):
            return ctx.enter_context(nc.semaphore(name))

        def sb(name, shape, dt=F32, scope=ctx):
            return scope.enter_context(nc.sbuf_tensor(name, shape, dt))

        banks = [ctx.enter_context(nc.psum_tensor(f"bank{n}", [P, NT], F32)) for n in range(8)]
        bank_q, bank_k, bank_g, bank_v, bank_s, bank_o, bank_x0, bank_x1 = banks
        bank_out = [bank_x0, bank_x1]
        bank_f = [bank_s, bank_o, bank_x0, bank_x1]

        acc = sb("acc", [P, KH, TOK])
        hx_hi = sb("hx_hi", [P, KH, TOK], F32R)
        hx_lo = sb("hx_lo", [P, KH, TOK], F32R)
        sq_acc = sb("sq_acc", [P, TOK])
        const = sb("const", [P, 3])
        cidx = sb("cidx", [P, TILES], I32)
        lidx = sb("lidx", [P, BATCH], I32)
        lidxf = sb("lidxf", [P, BATCH])
        lmask = sb("lmask", [P, RK, BATCH])
        ones = sb("ones", [P, P])
        bias_sb = sb("bias_sb", [P, KH])
        asum = sb("asum", [P, KH])
        alpha = sb("alpha", [P, KH])

        att = ExitStack()
        raw = sb("raw", [P, 4, HID], F32, att)
        raw_v = sb("raw_v", [P, KH, 2 * D], F32, att)
        w_hi = sb("w_hi", [P, 2, 4, HID], F32R, att)
        w_lo = sb("w_lo", [P, 2, 4, HID], F32R, att)
        v_hi = sb("v_hi", [P, KH, 2 * D], F32R, att)
        v_lo = sb("v_lo", [P, KH, 2 * D], F32R, att)
        mb = sb("mb", [P, 2, P + 1], F32, att)
        qt = sb("qt", [P, NT], F32, att)
        kt = sb("kt", [P, NT], F32, att)
        vt = sb("vt", [P, TILES, 2 * D], F32, att)
        tg = sb("tg", [P, NT], F32, att)
        sq = sb("sq", [P, NT], F32, att)
        sm = sb("sm", [P, NT], F32, att)
        t1 = sb("t1", [P, NT], F32, att)
        go_hi = sb("go_hi", [P, NT], F32R, att)
        go_lo = sb("go_lo", [P, NT], F32R, att)
        gidx = sb("gidx", [P, TILES], U32, att)
        gath = sb("gath", [P, TILES, SEQ], F32, att)
        mixw = sb("mixw", [P, TILES, P], F32, att)
        att.close()

        ffn = ExitStack()
        td = sb("td", [P, RK, TOK], F32, ctx)
        lt = sb("lt", [P, 2 * RK, TOK], F32, ffn)
        aw = sb("aw", [P, 2, KH, RK * P], F32, ffn)
        fraw = sb("fraw", [P, FW_AT[-1]], F32, ffn)
        fb = sb("fb", [P, 2, 2 * RK, P], F32, ffn)
        fw_hi = sb("fw_hi", [P, 2, FW_AT[-1]], F32R, ffn)
        fw_lo = sb("fw_lo", [P, 2, FW_AT[-1]], F32R, ffn)
        sg = sq_acc[:, 0:NT]
        ft = sq_acc[:, NT:2 * NT]
        fa_hi = sb("fa_hi", [P, NT], F32R, ffn)
        fa_lo = sb("fa_lo", [P, NT], F32R, ffn)
        ffn.close()

        bdw = sb("bdw", [P, RK, HID])
        lin_tt = sb("lin_tt", [P, KH, HID])
        lin_nn = sb("lin_nn", [P, KH, HID])
        absw = sb("absw", [P, HID])
        sgn = sb("sgn", [P, KH, HID], F32R)
        y_hi = sb("y_hi", [P, 2, KH, NT], F32R)
        y_lo = sb("y_lo", [P, 2, KH, NT], F32R)
        res = sb("res", [P, 4, NT])

        ld_small, ld_ones, ld_gath = sem("ld_small"), sem("ones_set"), sem("ld_gath")
        ld_x = [sem(f"ld_x{c}") for c in range(NC)]
        ld_w = [sem(f"ld_w{p}") for p in range(4)]
        ld_v = sem("ld_v")
        ld_m = [sem(f"ld_m{p}") for p in range(2)]
        idx_done, mixw_zero, mixw_done = sem("idx_done"), sem("mixw_zero"), sem("mixw_done")
        mix_done, mix_hi, mix_lo = sem("mix_done"), sem("mix_hi"), sem("mix_lo")
        acc_zero = sem("acc_zero")
        wh_done, wl_done, vh_done, vl_done = sem("wh_done"), sem("wl_done"), sem("vh_done"), sem("vl_done")
        q_done, k_done, g_done, v_done = sem("q_done"), sem("k_done"), sem("g_done"), sem("v_done")
        s_done, o_done, out_done = sem("s_done"), sem("o_done"), sem("out_done")
        q_sil, k_sil, v_sil, g_tanh, sq_done = sem("q_sil"), sem("k_sil"), sem("v_sil"), sem("g_tanh"), sem("sq_done")
        s_masked, t1_done, goh_done, go_done = sem("s_masked"), sem("t1_done"), sem("goh_done"), sem("go_done")
        sq_added, out_acc = sem("sq_added"), sem("out_acc")
        ld_xt = [sem(f"ld_xt{c}") for c in range(NC)]
        ld_aw, lidxf_done, lmask_done = sem("ld_aw"), sem("lidxf_done"), sem("lmask_done")
        ss_done, ms_done, rec_done, rstd_done = sem("ss_done"), sem("ms_done"), sem("rec_done"), sem("rstd_done")
        nrm_done, x1_done, x1_hi, x1_lo = sem("nrm_done"), sem("x1_done"), sem("x1_hi"), sem("x1_lo")
        rank_done, rank_masked, facc_zero = sem("rank_done"), sem("rank_masked"), sem("facc_zero")
        ld_f = [sem(f"ld_f{p}") for p in range(4)]
        ld_fb = [sem(f"ld_fb{p}") for p in range(2)]
        fh_done, fl_done = sem("fh_done"), sem("fl_done")
        fg_done, fu_done, fo_done = sem("fg_done"), sem("fu_done"), sem("fo_done")
        fg_sil, fact_done, fah_done, fal_done, f_acc = sem("fg_sil"), sem("fact_done"), sem("fah_done"), sem("fal_done"), sem("f_acc")
        ld_bd, ld_lt, ld_ln = sem("ld_bd"), sem("ld_lt"), sem("ld_ln")
        sgn_done, abs_done, alpha_done = sem("sgn_done"), sem("abs_done"), sem("alpha_done")
        td_masked, bd_done, y_done, yh_done, yl_done = sem("td_masked"), sem("bd_done"), sem("y_done"), sem("yh_done"), sem("yl_done")
        lin_done, res_act, res_a, res_done = sem("lin_done"), sem("res_act"), sem("res_a"), sem("res_done")
        stored = [sem(f"stored{r}") for r in range(4)]

        def ck(c):
            return slice(c * NT, (c + 1) * NT)

        def col(n, w=P):
            return slice(n * w, (n + 1) * w)

        x_tiles = acc[:, :, :].rearrange("p k (a n) -> p (k a) n", n=HID)

        def three(pe, dst, w_h, w_l, x_h, x_l, first, last):
            pe.matmul(dst, w_h, x_h, start=first, stop=False)
            pe.matmul(dst, w_h, x_l, start=False, stop=False)
            return pe.matmul(dst, w_l, x_h, start=False, stop=last)

        block = ctx.enter_context(nc.Block())

        @block.sync
        def _(sp):
            sp.dma_start(cidx[:, :], cond_idx).then_inc(ld_small, 16)
            sp.dma_start(const[:, :], consts).then_inc(ld_small, 16)
            sp.dma_start(lidx[:, :], lora_idx).then_inc(ld_small, 16)
            sp.dma_start(bias_sb[:, :], bias).then_inc(ld_small, 16)
            for c in range(NC):
                sp.dma_start(x_tiles[:, c * TPC:(c + 1) * TPC, :],
                             x_tok[:, c * TPC:(c + 1) * TPC, :]).then_inc(ld_x[c], 16)
                if c == 0:
                    sp.dma_start(raw_v[:, :, :], v_w[0]).then_inc(ld_v, 16)
                    for p in range(4):
                        sp.dma_start(raw[:, p, :], head_w[0, p]).then_inc(ld_w[p], 16)

            def load_head(n):
                for p in range(4):
                    sp.wait_ge(wl_done, 4 * n + p - 3)
                    sp.dma_start(raw[:, p, :], head_w[bass.ds(n, 1), p].rearrange("a p n -> p (a n)")
                                 ).then_inc(ld_w[p], 16)

            load_head(1)
            with sp.Fori(1, HEADS // 2) as m:
                sp.wait_ge(vl_done, 2 * m)
                sp.dma_start(raw_v[:, :, :], v_w[bass.ds(m, 1)].rearrange("a p k n -> p (a k) n")
                             ).then_inc(ld_v, 16)
                load_head(2 * m)
                load_head(2 * m + 1)

            sp.wait_ge(out_acc, 4 * UNITS)
            sp.dma_start(aw[:, :, :, :], a_w).then_inc(ld_aw, 16)
            for c in range(NC):
                sp.dma_start(lt[:, :, ck(c)], x_t[:, :, ck(c)]).then_inc(ld_xt[c], 16)
            for p in range(4):
                sp.dma_start(fraw[:, FW_AT[p]:FW_AT[p + 1]], ffn_w[0, :, FW_AT[p]:FW_AT[p + 1]]
                             ).then_inc(ld_f[p], 16)
            with sp.Fori(1, FC) as f:
                for p in range(4):
                    sp.wait_ge(fl_done, 4 * f + p - 3)
                    sp.dma_start(fraw[:, FW_AT[p]:FW_AT[p + 1]],
                                 ffn_w[bass.ds(f, 1), :, FW_AT[p]:FW_AT[p + 1]].rearrange("a p n -> p (a n)")
                                 ).then_inc(ld_f[p], 16)

            sp.wait_ge(f_acc, FOUT * FUNITS)
            sp.dma_start(bdw[:, :, :], bdown_w).then_inc(ld_bd, 16)
            sp.dma_start(lin_nn[:, :, :], lin_n).then_inc(ld_ln, 16)
            sp.dma_start(lin_tt[:, :, :], lin_t).then_inc(ld_lt, 16)
            for n in range(NC * KH):
                c, o = n // KH, n % KH
                sp.wait_ge(res_done, n + 1)
                sp.dma_start(out[o, :, ck(c)], res[:, n % 4, :]).then_inc(stored[n % 4], 16)
            for r in range(4):
                sp.wait_ge(stored[r], 16 * NC * KH // 4)

        @block.gpsimd
        def _(pool):
            pool.memset(mixw[:, :, :], 0.0).then_inc(mixw_zero, 1)
            pool.memset(ones[:, :], 1.0).then_inc(ld_ones, 1)
            pool.memset(sq_acc[:, :], 0.0).then_inc(acc_zero, 1)
            pool.wait_ge(idx_done, 1)
            for t in range(TILES):
                pool.indirect_dma_start(gath[:, t, :], None, cond_w,
                                        bass.IndirectOffsetOnAxis(ap=gidx[:, t:t + 1], axis=0)
                                        ).then_inc(ld_gath, 16)

            def load_misc(n, par):
                pool.dma_start(mb[:, par, :], misc[bass.ds(n, 1)].rearrange("a p n -> p (a n)")
                               ).then_inc(ld_m[par], 16)

            load_misc(0, 0)
            load_misc(1, 1)
            pool.wait_ge(mix_done, NC * KH)
            pool.memset(acc[:, :, :], 0.0).then_inc(acc_zero, 1)
            with pool.Fori(1, HEADS // 2) as m:
                for par in range(2):
                    pool.wait_ge(go_done, 8 * m - 4 + 4 * par)
                    load_misc(2 * m + par, par)

            def load_fb(f, par):
                pool.dma_start(fb[:, par, :, :], b_w[bass.ds(f, 1)].rearrange("a p k n -> p (a k) n")
                               ).then_inc(ld_fb[par], 16)

            pool.wait_ge(out_acc, 4 * UNITS)
            pool.memset(td[:, :, :], 0.0).then_inc(facc_zero, 1)
            load_fb(0, 0)
            load_fb(1, 1)
            for c in range(NC):
                pool.wait_ge(rank_done, 2 * RK * (c + 1))
                pool.wait_ge(x1_lo, c + 1)
                pool.memset(acc[:, :, ck(c)], 0.0).then_inc(facc_zero, 1)
            with pool.Fori(1, FC // 2) as m:
                for par in range(2):
                    pool.wait_ge(fu_done, 8 * m - 4 + 4 * par)
                    load_fb(2 * m + par, par)
            pool.wait_ge(fu_done, 4 * (FC - 2))
            load_fb(FC - 1, 0)

        @block.tensor
        def _(pe):
            for n in range(NC * KH):
                c, k = n // KH, n % KH
                if k == 0:
                    pe.wait_ge(ld_x[c], 16)
                    pe.wait_ge(mixw_done, 4 * (c + 1))
                if n >= 4:
                    pe.wait_ge(mix_lo, n - 3)
                for t in range(TPC):
                    mm = pe.matmul(banks[n % 4][:, col(t)], x_tiles[:, c * TPC + t, col(k)],
                                   mixw[:, c * TPC + t, :], start=True, stop=True)
                mm.then_inc(mix_done, 1)

            def project(par, part, c, dst, done):
                for k in range(KH):
                    mm = three(pe, dst[:, :], w_hi[:, par, part, col(k)], w_lo[:, par, part, col(k)],
                               hx_hi[:, k, ck(c)], hx_lo[:, k, ck(c)], k == 0, k == KH - 1)
                mm.then_inc(done, 1)

            def project_v(c, half):
                for t in range(2 * half, 2 * half + 2):
                    at = col(c * TPC + t)
                    for k in range(KH):
                        mm = three(pe, bank_v[:, col(t % 2, 2 * D)], hx_hi[:, k, at], hx_lo[:, k, at],
                                   v_hi[:, k, :], v_lo[:, k, :], k == 0, k == KH - 1)
                mm.then_inc(v_done, 1)

            def attend(u, v, par, c):
                pe.wait_ge(s_masked, u + 1)
                pe.wait_ge(v_sil, 2 * v)
                wait(pe, t1_done, u)
                wait(pe, sq_done, u)
                for t in range(TPC):
                    mm = pe.matmul(bank_o[:, col(t)], vt[:, c * TPC + t, col(par)], sm[:, col(t)],
                                   start=True, stop=True)
                mm.then_inc(o_done, 1)

            def project_out(u, par, n):
                g = 4 * u + n
                if n == 0:
                    pe.wait_ge(go_done, u + 1)
                if not isinstance(g, int) or g > 1:
                    pe.wait_ge(out_acc, g - 1)
                three(pe, bank_out[n % 2][:, :], w_hi[:, par, O, col(n)], w_lo[:, par, O, col(n)],
                      go_hi[:, :], go_lo[:, :], True, True).then_inc(out_done, 1)

            def unit(i, j):
                u, c, par, h, m = 8 * i + j, j % 4, j // 4 % 2, 2 * i + j // 4, i + j // 8
                bc, bpar, bh, bm = (j - 1) % 4, (j - 1) // 4 % 2, 2 * i + (j - 1) // 4, i + (j - 1) // 8
                if par == 0:
                    if c == 0:
                        pe.wait_ge(vl_done, 2 * m + 2)
                    wait(pe, v_sil, 8 * m + 2 * c)
                    project_v(c, 0)
                if c == 0:
                    pe.wait_ge(wl_done, 4 * h + 1)
                wait(pe, q_sil, u)
                project(par, Q, c, bank_q, q_done)
                if j > 0:
                    attend(u - 1, 4 * bm + 1 + bc if bpar == 0 else 4 * bm + 4, bpar, bc)
                if par == 0:
                    pe.wait_ge(v_sil, 8 * m + 2 * c + 1)
                    project_v(c, 1)
                if c == 0:
                    pe.wait_ge(wl_done, 4 * h + 2)
                wait(pe, k_sil, u)
                project(par, K, c, bank_k, k_done)
                if c == 0:
                    pe.wait_ge(wl_done, 4 * h + 3)
                wait(pe, g_tanh, u)
                project(par, G, c, bank_g, g_done)
                if j > 0:
                    if bc == 0:
                        pe.wait_ge(wl_done, 4 * bh + 4)
                    project_out(u - 1, bpar, 0)
                    project_out(u - 1, bpar, 1)
                pe.wait_ge(q_sil, u + 1)
                pe.wait_ge(k_sil, u + 1)
                wait(pe, s_masked, u)
                for t in range(TPC):
                    mm = pe.matmul(bank_s[:, col(t)], kt[:, col(t)], qt[:, col(t)], start=True, stop=True)
                mm.then_inc(s_done, 1)
                if j > 0:
                    project_out(u - 1, bpar, 2)
                    project_out(u - 1, bpar, 3)

            pe.wait_ge(mix_lo, NC * KH)
            unit(0, 0)
            unit(0, 1)
            with pe.Fori(0, HEADS // 2 - 1) as i:
                for j in range(2, 10):
                    unit(i, j)
            for j in range(2, 8):
                unit(HEADS // 2 - 1, j)
            attend(UNITS - 1, 4 * (HEADS // 2), 1, NC - 1)
            for n in range(4):
                project_out(UNITS - 1, 1, n)

            pe.wait_ge(out_acc, 4 * UNITS)
            pe.wait_ge(ld_ones, 1)
            for c in range(NC):
                pe.matmul(banks[c][:, :], ones[:, :], sq_acc[:, ck(c)], start=True, stop=True
                          ).then_inc(ss_done, 1)
            pe.wait_ge(ld_aw, 16)
            for c in range(NC):
                pe.wait_ge(x1_done, c + 1)
                for r in range(2 * RK):
                    if c:
                        pe.wait_ge(rank_masked, 2 * RK * (c - 1) + r + 1)
                    for k in range(KH):
                        mm = pe.matmul(bank_f[r][:, :], aw[:, r // RK, k, col(r % RK)],
                                       acc[:, k, ck(c)], start=(k == 0), stop=(k == KH - 1))
                    mm.then_inc(rank_done, 1)

            def up_or_gate(par, part, c, dst, done):
                for k in range(KH):
                    at = slice(FW_AT[part] + k * P, FW_AT[part] + (k + 1) * P)
                    three(pe, dst[:, :], fw_hi[:, par, at], fw_lo[:, par, at],
                          hx_hi[:, k, ck(c)], hx_lo[:, k, ck(c)], k == 0, False)
                for r in range(RK):
                    mm = pe.matmul(dst[:, :], fb[:, par, part * RK + r, :], lt[:, part * RK + r, ck(c)],
                                   start=False, stop=(r == RK - 1))
                mm.then_inc(done, 1)

            def funit(i, j, front=True):
                u, c, par, f = 8 * i + j, j % 4, j // 4 % 2, 2 * i + j // 4
                bpar, bf = (j - 1) // 4 % 2, 2 * i + (j - 1) // 4

                def downs(ns):
                    for n in ns:
                        g = FOUT * (u - 1) + n
                        if n == 0:
                            pe.wait_ge(fal_done, u)
                            if (j - 1) % 4 == 0:
                                pe.wait_ge(fl_done, 4 * bf + 4)
                        if not isinstance(g, int) or g > 3:
                            pe.wait_ge(f_acc, g - 3)
                        at = slice(FW_AT[2] + n * P, FW_AT[2] + (n + 1) * P)
                        three(pe, bank_f[(FOUT * (j - 1) + n) % 4][:, :], fw_hi[:, bpar, at],
                              fw_lo[:, bpar, at], fa_hi[:, :], fa_lo[:, :], True, True
                              ).then_inc(fo_done, 1)

                if front:
                    if c == 0:
                        pe.wait_ge(fl_done, 4 * f + 1)
                        pe.wait_ge(ld_fb[par], 16 * (i + j // 8) + 16)
                    wait(pe, fg_sil, u)
                    up_or_gate(par, 0, c, bank_q, fg_done)
                if j > 0:
                    downs(range(3))
                if front:
                    if c == 0:
                        pe.wait_ge(fl_done, 4 * f + 2)
                    wait(pe, fact_done, u)
                    up_or_gate(par, 1, c, bank_k, fu_done)
                if j > 0:
                    downs(range(3, FOUT))

            pe.wait_ge(rank_masked, 2 * RK * NC)
            pe.wait_ge(x1_lo, NC)
            funit(0, 0)
            funit(0, 1)
            with pe.Fori(0, FC // 2 - 1) as i:
                for j in range(2, 10):
                    funit(i, j)
            for j in range(2, 13):
                funit(FC // 2 - 1, j, front=j < 12)

            def bdown(c):
                pe.wait_ge(td_masked, c + 1)
                for o in range(KH):
                    n = KH * c + o
                    if n >= 4:
                        pe.wait_ge(y_done, n - 3)
                    for r in range(RK):
                        mm = pe.matmul(banks[n % 4][:, :], bdw[:, r, col(o)], td[:, r, ck(c)],
                                       start=(r == 0), stop=(r == RK - 1))
                    mm.then_inc(bd_done, 1)

            def linear(c):
                pe.wait_ge(yl_done, KH * (c + 1))
                for o in range(KH):
                    n = KH * c + o
                    if n >= 4:
                        pe.wait_ge(res_act, n - 3)
                    for k in range(KH):
                        pe.matmul(banks[4 + n % 4][:, :], sgn[:, k, col(o)], y_hi[:, c % 2, k, :],
                                  start=(k == 0), stop=False)
                        mm = pe.matmul(banks[4 + n % 4][:, :], sgn[:, k, col(o)], y_lo[:, c % 2, k, :],
                                       start=False, stop=(k == KH - 1))
                    mm.then_inc(lin_done, 1)

            pe.wait_ge(f_acc, FOUT * FUNITS)
            pe.wait_ge(ld_bd, 16)
            bdown(0)
            pe.wait_ge(sgn_done, KH)
            for c in range(NC):
                if c + 1 < NC:
                    bdown(c + 1)
                linear(c)

        @block.scalar
        def _(act):
            def head_hi(n, p, par):
                act.wait_ge(ld_w[p], 16 * n + 16)
                act.activation(w_hi[:, par, p, :], raw[:, p, :], ACT.Copy).then_inc(wh_done, 1)

            def v_hi_half(m, half):
                if half == 0:
                    act.wait_ge(ld_v, 16 * m + 16)
                at = slice(2 * half, 2 * half + 2)
                act.activation(v_hi[:, at, :], raw_v[:, at, :], ACT.Copy).then_inc(vh_done, 1)

            v_hi_half(0, 0)
            v_hi_half(0, 1)
            for p in range(4):
                head_hi(0, p, 0)
            for n in range(NC * KH):
                c, k = n // KH, n % KH
                act.wait_ge(mix_done, n + 1)
                act.activation(hx_hi[:, k, ck(c)], banks[n % 4][:, :], ACT.Copy).then_inc(mix_hi, 1)

            def silu_v(u_v, c, half):
                act.wait_ge(v_done, 2 * u_v + half + 1)
                act.activation(vt[:, c * TPC + 2 * half:c * TPC + 2 * half + 2, :],
                               bank_v[:, :].rearrange("p (t n) -> p t n", t=2), ACT.Silu).then_inc(v_sil, 1)

            def square(u):
                act.wait_ge(o_done, u + 1)
                wait(act, sq_added, u)
                act.activation(sq[:, :], bank_o[:, :], ACT.Square).then_inc(sq_done, 1)

            def unit(i, j, ahead=True):
                u, c, par, h, m = 8 * i + j, j % 4, j // 4 % 2, 2 * i + j // 4, i + j // 8
                if par == 0:
                    silu_v(4 * m + c, c, 0)
                act.wait_ge(q_done, u + 1)
                act.activation(qt[:, :], bank_q[:, :], ACT.Silu).then_inc(q_sil, 1)
                if j > 0:
                    square(u - 1)
                if par == 0:
                    silu_v(4 * m + c, c, 1)
                act.wait_ge(k_done, u + 1)
                act.activation(kt[:, :], bank_k[:, :], ACT.Silu).then_inc(k_sil, 1)
                act.wait_ge(g_done, u + 1)
                wait(act, t1_done, u)
                act.activation(tg[:, :], bank_g[:, :], ACT.Tanh, scale=0.5).then_inc(g_tanh, 1)
                if ahead:
                    head_hi(h + 1, c, 1 - par)
                    if par == 1 and c < 2:
                        v_hi_half(m + 1, c)

            unit(0, 0)
            unit(0, 1)
            with act.Fori(0, HEADS // 2 - 1) as i:
                for j in range(2, 10):
                    unit(i, j)
            for j in range(2, 8):
                unit(HEADS // 2 - 1, j, ahead=j < 4)
            square(UNITS - 1)

            for c in range(NC):
                act.wait_ge(rec_done, c + 1)
                act.activation(sq_acc[:, ck(c)], sq_acc[:, ck(c)], ACT.Sqrt).then_inc(rstd_done, 1)
            for c in range(NC):
                act.wait_ge(x1_done, c + 1)
                act.activation(hx_hi[:, :, ck(c)], acc[:, :, ck(c)], ACT.Copy).then_inc(x1_hi, 1)

            def ffn_hi(f, p, par):
                act.wait_ge(ld_f[p], 16 * f + 16)
                at = slice(FW_AT[p], FW_AT[p + 1])
                act.activation(fw_hi[:, par, at], fraw[:, at], ACT.Copy).then_inc(fh_done, 1)

            def funit(i, j, ahead=True):
                u, c, par, f = 8 * i + j, j % 4, j // 4 % 2, 2 * i + j // 4
                act.wait_ge(fg_done, u + 1)
                wait(act, fact_done, u)
                act.activation(sg, bank_q[:, :], ACT.Silu).then_inc(fg_sil, 1)
                if ahead:
                    ffn_hi(f + 1, c, 1 - par)
                act.wait_ge(fact_done, u + 1)
                act.activation(fa_hi[:, :], ft, ACT.Copy).then_inc(fah_done, 1)

            for p in range(4):
                ffn_hi(0, p, 0)
            funit(0, 0)
            funit(0, 1)
            with act.Fori(0, FC // 2 - 1) as i:
                for j in range(2, 10):
                    funit(i, j)
            for j in range(2, 12):
                funit(FC // 2 - 1, j, ahead=j < 8)

            act.wait_ge(f_acc, FOUT * FUNITS)
            act.wait_ge(ld_ln, 16)
            for o in range(KH):
                if o:
                    act.wait_ge(abs_done, o)
                act.activation(absw[:, :], lin_nn[:, o, :], ACT.Abs,
                               accum_out=asum[:, o:o + 1]).then_inc(abs_done, 1)
            act.wait_ge(ld_lt, 16)
            for k in range(KH):
                act.activation(sgn[:, k, :], lin_tt[:, k, :], ACT.Sign).then_inc(sgn_done, 1)

            def y_his(c):
                for o in range(KH):
                    n = KH * c + o
                    act.wait_ge(y_done, n + 1)
                    if c >= 2 and o == 0:
                        act.wait_ge(lin_done, KH * (c - 1))
                    act.activation(y_hi[:, c % 2, o, :], acc[:, o, ck(c)], ACT.Copy).then_inc(yh_done, 1)

            y_his(0)
            for c in range(NC):
                if c + 1 < NC:
                    y_his(c + 1)
                if c == 0:
                    act.wait_ge(alpha_done, 1)
                for o in range(KH):
                    n = KH * c + o
                    act.wait_ge(lin_done, n + 1)
                    if n >= 4:
                        act.wait_ge(stored[n % 4], 16 * (n // 4))
                    act.activation(res[:, n % 4, :], banks[4 + n % 4][:, :], ACT.Identity,
                                   scale=alpha[:, o:o + 1], bias=bias_sb[:, o:o + 1]).then_inc(res_act, 1)

        @block.vector
        def _(dve):
            dve.wait_ge(ld_small, 64)
            dve.tensor_scalar(gidx[:, :], cidx[:, :], float(SEQ), const[:, 0:1], ALU.mult, ALU.add
                              ).then_inc(idx_done, 1)
            dve.tensor_copy(lidxf[:, :], lidx[:, :]).then_inc(lidxf_done, 1)
            dve.wait_ge(lidxf_done, 1)
            for r in range(RK):
                dve.tensor_scalar(lmask[:, r, :], lidxf[:, :], const[:, 1 + r:2 + r], 0.5,
                                  ALU.is_equal, ALU.mult).then_inc(lmask_done, 1)

            def head_lo(n, p, par):
                dve.wait_ge(wh_done, 4 * n + p + 1)
                dve.tensor_tensor(w_lo[:, par, p, :], raw[:, p, :], w_hi[:, par, p, :].bitcast(F32),
                                  ALU.subtract).then_inc(wl_done, 1)

            def v_lo_half(m, half):
                dve.wait_ge(vh_done, 2 * m + half + 1)
                at = slice(2 * half, 2 * half + 2)
                dve.tensor_tensor(v_lo[:, at, :], raw_v[:, at, :], v_hi[:, at, :].bitcast(F32),
                                  ALU.subtract).then_inc(vl_done, 1)

            dve.wait_ge(mixw_zero, 1)
            for c in range(NC):
                ts = slice(c * TPC, (c + 1) * TPC)
                dve.wait_ge(ld_gath, 16 * TILES)
                for b in range(4):
                    rows = slice(SEQ * b, SEQ * (b + 1))
                    dve.tensor_copy(mixw[rows, ts, rows], gath[rows, ts, :]).then_inc(mixw_done, 1)
            v_lo_half(0, 0)
            v_lo_half(0, 1)
            for p in range(4):
                head_lo(0, p, 0)
            for n in range(NC * KH):
                c, k = n // KH, n % KH
                dve.wait_ge(mix_hi, n + 1)
                dve.tensor_tensor(hx_lo[:, k, ck(c)], banks[n % 4][:, :], hx_hi[:, k, ck(c)].bitcast(F32),
                                  ALU.subtract).then_inc(mix_lo, 1)

            def mask_s(u, par):
                dve.wait_ge(s_done, u + 1)
                dve.tensor_tensor(sm[:, :].rearrange("p (t n) -> p t n", t=TPC),
                                  bank_s[:, :].rearrange("p (t n) -> p t n", t=TPC),
                                  mb[:, par, 0:P].unsqueeze(1).to_broadcast([P, TPC, P]),
                                  ALU.mult).then_inc(s_masked, 1)

            def gate_o(u, par, c):
                dve.wait_ge(g_tanh, u + 1)
                dve.wait_ge(sq_done, u + 1)
                dve.scalar_tensor_tensor(out=t1[:, :], in0=tg[:, :], scalar=1.0, in1=bank_o[:, :],
                                         op0=ALU.add, op1=ALU.mult).then_inc(t1_done, 1)
                dve.wait_ge(t1_done, u + 1)
                dve.tensor_scalar(go_hi[:, :], t1[:, :], mb[:, par, P:P + 1], None, ALU.mult
                                  ).then_inc(goh_done, 1)
                dve.wait_ge(goh_done, u + 1)
                dve.scalar_tensor_tensor(out=go_lo[:, :], in0=t1[:, :], scalar=mb[:, par, P:P + 1],
                                         in1=go_hi[:, :].bitcast(F32), op0=ALU.mult, op1=ALU.subtract
                                         ).then_inc(go_done, 1)
                dve.tensor_tensor(sq_acc[:, ck(c)], sq_acc[:, ck(c)], sq[:, :], ALU.add
                                  ).then_inc(sq_added, 1)

            def add_out(u, c, n):
                dve.wait_ge(out_done, 4 * u + n + 1)
                dve.tensor_tensor(acc[:, n, ck(c)], acc[:, n, ck(c)], bank_out[n % 2][:, :], ALU.add
                                  ).then_inc(out_acc, 1)

            def unit(i, j, ahead=True):
                u, c, par, h, m = 8 * i + j, j % 4, j // 4 % 2, 2 * i + j // 4, i + j // 8
                bc, bpar = (j - 1) % 4, (j - 1) // 4 % 2
                if j > 0:
                    gate_o(u - 1, bpar, bc)
                if ahead:
                    head_lo(h + 1, c, 1 - par)
                    if par == 1 and c < 2:
                        v_lo_half(m + 1, c)
                if j > 0:
                    add_out(u - 1, bc, 0)
                    add_out(u - 1, bc, 1)
                if c == 0:
                    dve.wait_ge(ld_m[par], 16 * (i + j // 8) + 16)
                mask_s(u, par)
                if j > 0:
                    add_out(u - 1, bc, 2)
                    add_out(u - 1, bc, 3)

            dve.wait_ge(acc_zero, 2)
            unit(0, 0)
            unit(0, 1)
            with dve.Fori(0, HEADS // 2 - 1) as i:
                for j in range(2, 10):
                    unit(i, j)
            for j in range(2, 8):
                unit(HEADS // 2 - 1, j, ahead=j < 4)
            gate_o(UNITS - 1, 1, NC - 1)
            for n in range(4):
                add_out(UNITS - 1, NC - 1, n)

            for c in range(NC):
                dve.wait_ge(ss_done, c + 1)
                dve.tensor_scalar(sq_acc[:, ck(c)], banks[c][:, :], 4.0 / HD, EPS, ALU.mult, ALU.add
                                  ).then_inc(ms_done, 1)
                dve.wait_ge(ms_done, c + 1)
                dve.reciprocal(sq_acc[:, ck(c)], sq_acc[:, ck(c)]).then_inc(rec_done, 1)

            def mask_ranks(dst, src, r, c):
                return dve.tensor_tensor(dst.rearrange("p (b s) -> p b s", s=SEQ),
                                         src.rearrange("p (b s) -> p b s", s=SEQ),
                                         lmask[:, r, c * BPC:(c + 1) * BPC].unsqueeze(2)
                                         .to_broadcast([P, BPC, SEQ]), ALU.mult)

            dve.wait_ge(lmask_done, RK)
            for c in range(NC):
                dve.wait_ge(rstd_done, c + 1)
                dve.tensor_tensor(acc[:, :, ck(c)], acc[:, :, ck(c)],
                                  sq_acc[:, ck(c)].unsqueeze(1).to_broadcast([P, KH, NT]), ALU.mult
                                  ).then_inc(nrm_done, 1)
                dve.wait_ge(nrm_done, c + 1)
                dve.wait_ge(ld_xt[c], 16)
                dve.tensor_tensor(acc[:, :, ck(c)], acc[:, :, ck(c)], lt[:, :, ck(c)], ALU.add
                                  ).then_inc(x1_done, 1)
                dve.wait_ge(x1_hi, c + 1)
                dve.tensor_tensor(hx_lo[:, :, ck(c)], acc[:, :, ck(c)], hx_hi[:, :, ck(c)].bitcast(F32),
                                  ALU.subtract).then_inc(x1_lo, 1)
                for r in range(2 * RK):
                    dve.wait_ge(rank_done, 2 * RK * c + r + 1)
                    mask_ranks(lt[:, r, ck(c)], bank_f[r][:, :], r % RK, c).then_inc(rank_masked, 1)

            def ffn_lo(f, p, par):
                dve.wait_ge(fh_done, 4 * f + p + 1)
                at = slice(FW_AT[p], FW_AT[p + 1])
                dve.tensor_tensor(fw_lo[:, par, at], fraw[:, at], fw_hi[:, par, at].bitcast(F32),
                                  ALU.subtract).then_inc(fl_done, 1)

            def add_down(u, j, n):
                c = j % 4
                dve.wait_ge(fo_done, FOUT * u + n + 1)
                dst = acc[:, n, ck(c)] if n < KH else td[:, n - KH, ck(c)]
                dve.tensor_tensor(dst, dst, bank_f[(FOUT * j + n) % 4][:, :], ALU.add).then_inc(f_acc, 1)

            def funit(i, j, front=True, ahead=True):
                u, c, par, f = 8 * i + j, j % 4, j // 4 % 2, 2 * i + j // 4
                if j > 0:
                    for n in range(3):
                        add_down(u - 1, j - 1, n)
                if ahead:
                    ffn_lo(f + 1, c, 1 - par)
                if j > 0:
                    for n in range(3, FOUT):
                        add_down(u - 1, j - 1, n)
                if front:
                    dve.wait_ge(fu_done, u + 1)
                    dve.wait_ge(fg_sil, u + 1)
                    dve.tensor_tensor(ft, sg, bank_k[:, :], ALU.mult).then_inc(fact_done, 1)
                    dve.wait_ge(fah_done, u + 1)
                    dve.tensor_tensor(fa_lo[:, :], ft, fa_hi[:, :].bitcast(F32), ALU.subtract
                                      ).then_inc(fal_done, 1)

            for p in range(4):
                ffn_lo(0, p, 0)
            dve.wait_ge(facc_zero, 1 + NC)
            funit(0, 0)
            funit(0, 1)
            with dve.Fori(0, FC // 2 - 1) as i:
                for j in range(2, 10):
                    funit(i, j)
            for j in range(2, 13):
                funit(FC // 2 - 1, j, front=j < 12, ahead=j < 8)

            dve.wait_ge(abs_done, KH)
            dve.tensor_scalar(alpha[:, :], asum[:, :], 1.0 / HID, None, ALU.mult).then_inc(alpha_done, 1)
            for c in range(NC):
                for r in range(RK):
                    m = mask_ranks(td[:, r, ck(c)], td[:, r, ck(c)], r, c)
                m.then_inc(td_masked, 1)

            def y_los(c):
                for o in range(KH):
                    n = KH * c + o
                    dve.wait_ge(bd_done, n + 1)
                    dve.tensor_tensor(acc[:, o, ck(c)], acc[:, o, ck(c)], banks[n % 4][:, :], ALU.add
                                      ).then_inc(y_done, 1)
                for o in range(KH):
                    n = KH * c + o
                    dve.wait_ge(yh_done, n + 1)
                    dve.tensor_tensor(y_lo[:, c % 2, o, :], acc[:, o, ck(c)],
                                      y_hi[:, c % 2, o, :].bitcast(F32), ALU.subtract).then_inc(yl_done, 1)

            y_los(0)
            for c in range(NC):
                if c + 1 < NC:
                    y_los(c + 1)
                for o in range(KH):
                    n = KH * c + o
                    r = res[:, n % 4, :]
                    dve.wait_ge(res_act, n + 1)
                    dve.tensor_tensor(r, r, hx_hi[:, o, ck(c)].bitcast(F32), ALU.add).then_inc(res_a, 1)
                    dve.wait_ge(res_a, n + 1)
                    dve.tensor_tensor(r, r, hx_lo[:, o, ck(c)].bitcast(F32), ALU.add).then_inc(res_done, 1)


def decay_masks():
    layer, layers = 1, 32
    base = np.float32(1.0 / 2.0 ** (8.0 / HEADS))
    factor = np.float32(1.0 - layer / (layers - 1 + 1e-05) + 1e-05)
    slope = base ** (np.arange(HEADS, dtype=np.float32) + 1) * factor
    diff = np.arange(SEQ)[None, :] - np.arange(SEQ)[:, None]
    one = np.where(diff >= 0, np.exp(-slope[:, None, None] * np.maximum(diff, 0)), 0.0) * 0.5
    full = np.zeros((HEADS, P, P), np.float32)
    for b in range(P // SEQ):
        full[:, b * SEQ:(b + 1) * SEQ, b * SEQ:(b + 1) * SEQ] = one
    return full


def kernel(**inputs):
    import concourse.bacc as bacc
    from concourse.bass_utils import run_bass_kernel_spmd

    x = np.asarray(inputs["x"])
    cond = np.asarray(inputs["itok_B_0_15"]).astype(np.int32)
    lora = np.asarray(inputs["itok_B_2_6"]).astype(np.int32)

    def chunked(w):
        return np.asarray(w).reshape(-1, KH, P).transpose(2, 1, 0)

    qkv = np.asarray(inputs["L0_attn_qkv_w"]).reshape(HEADS, 3, D, KH, P)
    by_head = qkv.transpose(0, 1, 4, 3, 2)
    gate = np.asarray(inputs["L0_attn_gate_w"]).reshape(HEADS, D, KH, P).transpose(0, 3, 2, 1)
    outw = np.asarray(inputs["L0_attn_out_w"]).reshape(HID, HEADS, D).transpose(1, 2, 0)
    head_w = np.stack([by_head[:, 0].reshape(HEADS, P, HID), by_head[:, 1].reshape(HEADS, P, HID),
                       gate.reshape(HEADS, P, HID), outw], 1)
    v_w = by_head[:, 2].reshape(HEADS // 2, 2, P, KH, D).transpose(0, 2, 3, 1, 4).reshape(
        HEADS // 2, P, KH, 2 * D)
    norm = np.asarray(inputs["L0_attn_norm_w"]).reshape(HEADS, D, 1)
    misc = np.concatenate([decay_masks(), norm], 2)

    def padded(w, axis):
        shape = list(w.shape)
        shape[axis] = FC * P - F
        return np.concatenate([w, np.zeros(shape, w.dtype)], axis)

    def hidden(w):
        return padded(np.asarray(w), 0).reshape(FC, P, KH, P).transpose(0, 3, 2, 1).reshape(FC, P, HID)

    downw = padded(np.asarray(inputs["L0_cond2_W_down"]), 1).reshape(HID, FC, P).transpose(1, 2, 0)
    adown = padded(np.asarray(inputs["L0_cond2_A_down"])[0], 2).reshape(CONDS * RANK, FC, P).transpose(1, 2, 0)
    ffn_w = np.concatenate([hidden(inputs["L0_cond2_W_gate"]), hidden(inputs["L0_cond2_W_up"]),
                            downw, adown], 2)

    def ranks(w):
        w = padded(np.asarray(w)[0], 1).transpose(0, 2, 1).reshape(RK, P, FC, P)
        return w.transpose(2, 1, 0, 3)

    b_w = np.concatenate([ranks(inputs["L0_cond2_B_gate"]), ranks(inputs["L0_cond2_B_up"])], 2)
    a_w = np.stack([chunked(np.asarray(inputs[n])[0].reshape(CONDS * RANK, HID))
                    for n in ("L0_cond2_A_gate", "L0_cond2_A_up")], 1)
    bdown = np.asarray(inputs["L0_cond2_B_down"])[0].transpose(0, 2, 1).reshape(RK, P, HID).transpose(1, 0, 2)
    lin = np.asarray(inputs["L0_ffn_weight_real"])
    rows = np.arange(P)
    consts = np.stack([rows % SEQ, rows // RANK, rows // RANK + P // RANK], 1).astype(np.float32)
    arrays = dict(
        x_tok=x.reshape(TILES, P, HID).transpose(1, 0, 2),
        x_t=chunked(x.reshape(TOK, HID)),
        cond_idx=np.repeat(cond.reshape(TILES, 4).T, SEQ, 0),
        lora_idx=np.repeat(lora.reshape(1, BATCH), P, 0),
        consts=consts,
        cond_w=np.asarray(inputs["L0_cond_weights"]).reshape(CONDS * SEQ, SEQ),
        head_w=head_w, v_w=v_w, misc=misc, a_w=a_w, ffn_w=ffn_w, b_w=b_w, bdown_w=bdown,
        lin_t=chunked(lin),
        lin_n=lin.reshape(KH, P, HID).transpose(1, 0, 2),
        bias=np.asarray(inputs["L0_ffn_bias"]).reshape(KH, P).T,
    )
    arrays = {n: np.ascontiguousarray(a) for n, a in arrays.items()}
    nc = bacc.Bacc("TRN2", target_bir_lowering=False, num_devices=1)
    args = {n: nc.dram_tensor(n + "_dram", a.shape, mybir.dt.from_np(a.dtype), kind="ExternalInput").ap()
            for n, a in arrays.items()}
    out = nc.dram_tensor("out_dram", (KH, P, TOK), F32, kind="ExternalOutput").ap()
    build(nc, *args.values(), out)
    r = run_bass_kernel_spmd(nc, [{n + "_dram": a for n, a in arrays.items()}], core_ids=[0])
    got = np.asarray(r.results[0]["out_dram"])
    return got.reshape(HID, TOK).T.reshape(BATCH, SEQ, HID)
```

```python
from contextlib import ExitStack

import numpy as np

import concourse.bass as bass
from concourse import mybir

F32 = mybir.dt.float32
F32R = mybir.dt.float32r
I32 = mybir.dt.int32
U32 = mybir.dt.uint32
ALU = mybir.AluOpType
ACT = mybir.ActivationFunctionType

P = 128
BATCH, SEQ, HID = 64, 32, 512
TOK = BATCH * SEQ
KH = HID // P
NT = 512
NC = TOK // NT
TILES = TOK // P
TPC = NT // P
BPC = NT // SEQ
HEADS, D = 32, 128
CONDS, RANK = 16, 16
RK = CONDS * RANK // P
F = 1376
FC = -(-F // P)
EPS = 1e-5
HD = HEADS * D
UNITS = HEADS * NC
FUNITS = FC * NC
Q, K, G, O = range(4)
FOUT = KH + RK
GB = P // RANK
GT = GB * SEQ
NG = TOK // GT
GPC = NT // GT
LAST = UNITS - NC
FW_AT = [0, 512, 1024, 1536, 1792]


def wait(eng, sem, value):
    if not isinstance(value, int) or value > 0:
        eng.wait_ge(sem, value)


def build(nc, x_tok, x_t, cond_idx, lora_idx, rank_idx, consts, eye, cond_w, head_w, v_w, misc, a_w,
          ffn_w, b_w, bdown_w, lin_t, bias, out):
    with ExitStack() as ctx:
        def sem(name):
            return ctx.enter_context(nc.semaphore(name))

        def sb(name, shape, dt=F32, scope=ctx):
            return scope.enter_context(nc.sbuf_tensor(name, shape, dt))

        banks = [ctx.enter_context(nc.psum_tensor(f"bank{n}", [P, NT], F32)) for n in range(8)]
        bank_q, bank_k, bank_g, bank_v, bank_s, bank_o, bank_x0, bank_x1 = banks
        bank_out = [bank_x0, bank_x1]
        bank_f = [bank_s, bank_o, bank_x0, bank_x1]

        acc = sb("acc", [P, KH, TOK])
        hx_hi = sb("hx_hi", [P, KH, TOK], F32R)
        hx_lo = sb("hx_lo", [P, KH, TOK], F32R)
        sq_acc = sb("sq_acc", [P, TOK])
        const = sb("const", [P, 4 + GB])
        cidx = sb("cidx", [P, TILES], I32)
        lidx = sb("lidx", [P, BATCH], I32)
        lidxf = sb("lidxf", [P, BATCH])
        lmask = sb("lmask", [P, RK, BATCH])
        ridx = sb("ridx", [P, NG], I32)
        fidx = sb("fidx", [P, 2, NG], U32)
        fstep = sb("fstep", [P, NG], U32)
        aidx = sb("aidx", [P, NG], U32)
        ones = sb("ones", [P, P])
        ident = sb("ident", [P, P])
        bias_sb = sb("bias_sb", [P, KH])
        alpha = sb("alpha", [P, KH])

        att = ExitStack()
        v_hi = sb("v_hi", [P, KH, 2 * D], F32R, att)
        v_lo = sb("v_lo", [P, KH, 2 * D], F32R, att)
        raw_v = sb("raw_v", [P, KH, 2 * D], F32, att)
        raw = sb("raw", [P, 4, HID], F32, att)
        w_hi, w_lo = [None, None], [None, None]
        w_hi[0] = sb("w_hi0", [P, 4, HID], F32R, att)
        w_lo[0] = sb("w_lo0", [P, 4, HID], F32R, att)
        mixw = sb("mixw", [P, TILES, P], F32, att)
        gath = sb("gath", [P, TILES, 2 * SEQ], F32, att)
        w_hi[1] = sb("w_hi1", [P, 4, HID], F32R, att)
        w_lo[1] = sb("w_lo1", [P, 4, HID], F32R, att)
        mb = sb("mb", [P, 2, P + 1], F32, att)
        qt = sb("qt", [P, NT], F32, att)
        kt = sb("kt", [P, NT], F32, att)
        vt = sb("vt", [P, TILES, 2 * D], F32, att)
        tg = sb("tg", [P, NT], F32, att)
        sq = sb("sq", [P, NT], F32, att)
        sm = sb("sm", [P, NT], F32, att)
        t1 = sb("t1", [P, NT], F32, att)
        go_hi = sb("go_hi", [P, NT], F32R, att)
        go_lo = sb("go_lo", [P, NT], F32R, att)
        gidx = sb("gidx", [P, TILES], U32, att)
        att.close()

        lt = sb("lt", [P, 4, TOK])
        fb = [lt[:, 2 + par, :].rearrange("p (g n) -> p g n", g=NG) for par in range(2)]
        td = sb("td", [P, RK, TOK])
        ag = td[:, 0, :].rearrange("p (b n) -> p b n", b=2)
        agt = td[:, 1, :].rearrange("p (b n) -> p b n", b=2)
        bdw = sb("bdw", [P, RK, HID])
        lin_tt = sb("lin_tt", [P, KH, HID])
        ffn = ExitStack()
        fraw = sb("fraw", [P, FW_AT[-1]], F32, ffn)
        fw_hi = sb("fw_hi", [P, 2, FW_AT[-1]], F32R, ffn)
        fw_lo = sb("fw_lo", [P, 2, FW_AT[-1]], F32R, ffn)
        fa_hi = sb("fa_hi", [P, NT], F32R, ffn)
        fa_lo = sb("fa_lo", [P, NT], F32R, ffn)
        sg = sq_acc[:, 0:NT]
        ft = sq_acc[:, NT:2 * NT]
        ffn.close()

        sgn = sb("sgn", [P, KH, HID], F32R)
        y_hi = sb("y_hi", [P, 2, KH, NT], F32R)
        y_lo = sb("y_lo", [P, 2, KH, NT], F32R)
        res = lt[:, 0, :].rearrange("p (r n) -> p r n", r=4)
        absw = lt[:, 1, :].rearrange("p (k n) -> p k n", k=KH)

        ld_small, ones_set, ld_late = sem("ld_small"), sem("ones_set"), sem("ld_late")
        ld_gath = [sem(f"ld_gath{c}") for c in range(NC)]
        ld_x = [sem(f"ld_x{c}") for c in range(NC)]
        ld_w = [sem(f"ld_w{p}") for p in range(4)]
        ld_v = sem("ld_v")
        ld_m = [sem(f"ld_m{p}") for p in range(2)]
        idx_done, mixw_zero, mixw_done = sem("idx_done"), sem("mixw_zero"), sem("mixw_done")
        mix_done, mix_hi, mix_lo = sem("mix_done"), sem("mix_hi"), sem("mix_lo")
        acc_zero = sem("acc_zero")
        wh_done, wl_done, vh_done, vl_done = sem("wh_done"), sem("wl_done"), sem("vh_done"), sem("vl_done")
        q_done, k_done, g_done, v_done = sem("q_done"), sem("k_done"), sem("g_done"), sem("v_done")
        s_done, o_done, out_done = sem("s_done"), sem("o_done"), sem("out_done")
        q_sil, k_sil, v_sil, g_tanh, sq_done = sem("q_sil"), sem("k_sil"), sem("v_sil"), sem("g_tanh"), sem("sq_done")
        s_masked, t1_done, goh_done, go_done = sem("s_masked"), sem("t1_done"), sem("goh_done"), sem("go_done")
        sq_added, out_acc = sem("sq_added"), sem("out_acc")
        ld_xt = [sem(f"ld_xt{c}") for c in range(NC)]
        ld_ag = [sem(f"ld_ag{n}") for n in range(2)]
        lidxf_done, lmask_done, ridx_done = sem("lidxf_done"), sem("lmask_done"), sem("ridx_done")
        fidx_done, fidx_seen, at_done, at_copied = sem("fidx_done"), sem("fidx_seen"), sem("at_done"), sem("at_copied")
        ss_done, ms_done, rec_done, rstd_done = sem("ss_done"), sem("ms_done"), sem("rec_done"), sem("rstd_done")
        nrm_done, x1_done, x1_hi, x1_lo = sem("nrm_done"), sem("x1_done"), sem("x1_hi"), sem("x1_lo")
        rank_done, rank_masked, facc_zero = sem("rank_done"), sem("rank_masked"), sem("facc_zero")
        ld_f = [sem(f"ld_f{p}") for p in range(4)]
        ld_fb = [sem(f"ld_fb{p}") for p in range(2)]
        fh_done, fl_done = sem("fh_done"), sem("fl_done")
        fg_done, fu_done, fo_done = sem("fg_done"), sem("fu_done"), sem("fo_done")
        fg_sil, fact_done, fah_done, fal_done, f_acc = sem("fg_sil"), sem("fact_done"), sem("fah_done"), sem("fal_done"), sem("f_acc")
        ld_bd, ld_lt = sem("ld_bd"), sem("ld_lt")
        sgn_done, abs_done, asum_done, alpha_done = sem("sgn_done"), sem("abs_done"), sem("asum_done"), sem("alpha_done")
        td_masked, bd_done, y_done, yh_done, yl_done = sem("td_masked"), sem("bd_done"), sem("y_done"), sem("yh_done"), sem("yl_done")
        lin_done, res_act, res_a, res_done = sem("lin_done"), sem("res_act"), sem("res_a"), sem("res_done")
        stored = [sem(f"stored{r}") for r in range(4)]

        def ck(c):
            return slice(c * NT, (c + 1) * NT)

        def col(n, w=P):
            return slice(n * w, (n + 1) * w)

        x_tiles = acc[:, :, :].rearrange("p k (a n) -> p (k a) n", n=HID)

        def three(pe, dst, w_h, w_l, x_h, x_l, first, last):
            pe.matmul(dst, w_h, x_h, start=first, stop=False)
            pe.matmul(dst, w_h, x_l, start=False, stop=False)
            return pe.matmul(dst, w_l, x_h, start=False, stop=last)

        block = ctx.enter_context(nc.Block())

        @block.sync
        def _(sp):
            sp.dma_start(cidx[:, :], cond_idx).then_inc(ld_small, 16)
            sp.dma_start(const[:, :], consts).then_inc(ld_small, 16)

            def load_x(c):
                at = slice(c * TPC, (c + 1) * TPC)
                sp.dma_start(x_tiles[:, at, :], x_tok[:, at, :]).then_inc(ld_x[c], 16)

            load_x(0)
            load_x(1)
            sp.dma_start(raw_v[:, :, :], v_w[0]).then_inc(ld_v, 16)
            for p in range(4):
                sp.dma_start(raw[:, p, :], head_w[0, p]).then_inc(ld_w[p], 16)
            load_x(2)
            load_x(3)
            sp.dma_start(lidx[:, :], lora_idx).then_inc(ld_late, 16)
            sp.dma_start(ridx[:, :], rank_idx).then_inc(ld_late, 16)
            sp.dma_start(bias_sb[:, :], bias).then_inc(ld_late, 16)
            sp.dma_start(ident[:, :], eye).then_inc(ld_late, 16)

            def load_head(n):
                for p in range(4):
                    sp.wait_ge(wl_done, 4 * n + p - 3)
                    sp.dma_start(raw[:, p, :], head_w[bass.ds(n, 1), p].rearrange("a p n -> p (a n)")
                                 ).then_inc(ld_w[p], 16)

            load_head(1)
            with sp.Fori(1, HEADS // 2) as m:
                sp.wait_ge(vl_done, 2 * m)
                sp.dma_start(raw_v[:, :, :], v_w[bass.ds(m, 1)].rearrange("a p k n -> p (a k) n")
                             ).then_inc(ld_v, 16)
                load_head(2 * m)
                load_head(2 * m + 1)

            sp.wait_ge(out_acc, 4 * LAST)
            for c in range(NC):
                sp.dma_start(lt[:, :, ck(c)], x_t[:, :, ck(c)]).then_inc(ld_xt[c], 16)
            sp.wait_ge(out_acc, 4 * UNITS)
            for p in range(4):
                sp.dma_start(fraw[:, FW_AT[p]:FW_AT[p + 1]], ffn_w[0, :, FW_AT[p]:FW_AT[p + 1]]
                             ).then_inc(ld_f[p], 16)
            sp.dma_start(bdw[:, :, :], bdown_w).then_inc(ld_bd, 16)
            sp.dma_start(lin_tt[:, :, :], lin_t).then_inc(ld_lt, 16)
            with sp.Fori(1, FC) as f:
                for p in range(4):
                    sp.wait_ge(fl_done, 4 * f + p - 3)
                    sp.dma_start(fraw[:, FW_AT[p]:FW_AT[p + 1]],
                                 ffn_w[bass.ds(f, 1), :, FW_AT[p]:FW_AT[p + 1]].rearrange("a p n -> p (a n)")
                                 ).then_inc(ld_f[p], 16)

            for n in range(NC * KH):
                c, o = n // KH, n % KH
                sp.wait_ge(res_done, n + 1)
                sp.dma_start(out[o, :, ck(c)], res[:, n % 4, :]).then_inc(stored[n % 4], 16)
            for r in range(4):
                sp.wait_ge(stored[r], 16 * NC * KH // 4)

        @block.gpsimd
        def _(pool):
            pool.wait_ge(idx_done, 1)
            for t in range(TILES):
                pool.indirect_dma_start(gath[:, t, 0:SEQ], None, cond_w,
                                        bass.IndirectOffsetOnAxis(ap=gidx[:, t:t + 1], axis=0)
                                        ).then_inc(ld_gath[t // TPC], 16)
            pool.memset(ones[:, :], 1.0).then_inc(ones_set, 1)
            pool.memset(sq_acc[:, :], 0.0).then_inc(acc_zero, 1)

            def load_misc(n, par):
                pool.dma_start(mb[:, par, :], misc[bass.ds(n, 1)].rearrange("a p n -> p (a n)")
                               ).then_inc(ld_m[par], 16)

            load_misc(0, 0)
            load_misc(1, 1)
            pool.wait_ge(mix_done, NC * KH)
            pool.memset(acc[:, :, :], 0.0).then_inc(acc_zero, 1)
            with pool.Fori(1, HEADS // 2) as m:
                for par in range(2):
                    pool.wait_ge(go_done, 8 * m - 4 + 4 * par)
                    load_misc(2 * m + par, par)

            def gather_a(g):
                if g >= 2:
                    pool.wait_ge(at_done, g - 1)
                pool.indirect_dma_start(ag[:, g % 2, :], None, a_w,
                                        bass.IndirectOffsetOnAxis(ap=aidx[:, g:g + 1], axis=0)
                                        ).then_inc(ld_ag[g % 2], 16)

            def gather_fb(par):
                for g in range(NG):
                    pool.indirect_dma_start(fb[par][:, g, :], None, b_w,
                                            bass.IndirectOffsetOnAxis(ap=fidx[:, par, g:g + 1], axis=0)
                                            ).then_inc(ld_fb[par], 16)

            def split_x1(c):
                pool.wait_ge(x1_hi, c + 1)
                pool.tensor_tensor(hx_lo[:, :, ck(c)], acc[:, :, ck(c)], hx_hi[:, :, ck(c)].bitcast(F32),
                                   ALU.subtract).then_inc(x1_lo, 1)

            pool.wait_ge(ridx_done, 3)
            pool.wait_ge(out_acc, 4 * LAST)
            pool.memset(fstep[:, :], 2 * CONDS * RANK).then_inc(fidx_done, 1)
            gather_a(0)
            gather_a(1)
            for c in range(NC):
                if c == NC - 1:
                    pool.wait_ge(x1_done, NC)
                    gather_fb(0)
                split_x1(c)
                if c < NC - 1:
                    gather_a(2 * c + 2)
                    gather_a(2 * c + 3)
            gather_fb(1)
            pool.wait_ge(x1_lo, NC)
            for c in range(NC):
                pool.wait_ge(rank_done, GPC * (c + 1))
                pool.memset(acc[:, :, ck(c)], 0.0).then_inc(facc_zero, 1)
            pool.memset(td[:, :, :], 0.0).then_inc(facc_zero, 1)

            def next_fb(m, par):
                pool.wait_ge(fu_done, 8 * m - 4 + 4 * par)
                pool.tensor_tensor(fidx[:, par, :], fidx[:, par, :], fstep[:, :], ALU.add
                                   ).then_inc(fidx_done, 1)
                pool.wait_ge(fidx_done, 2 * m + par)
                pool.sem_inc(fidx_seen, 1)
                gather_fb(par)

            pool.wait_ge(fidx_done, 1)
            with pool.Fori(1, FC // 2) as m:
                next_fb(m, 0)
                next_fb(m, 1)
            next_fb(FC // 2, 0)

        @block.tensor
        def _(pe):
            for n in range(NC * KH):
                c, k = n // KH, n % KH
                if k == 0:
                    pe.wait_ge(ld_x[c], 16)
                    pe.wait_ge(mixw_done, 4 * (c + 1))
                if n >= 8:
                    pe.wait_ge(mix_lo, n - 7)
                for t in range(TPC):
                    mm = pe.matmul(banks[n % 8][:, col(t)], x_tiles[:, c * TPC + t, col(k)],
                                   mixw[:, c * TPC + t, :], start=True, stop=True)
                mm.then_inc(mix_done, 1)

            def project(par, part, c, dst, done):
                for k in range(KH):
                    mm = three(pe, dst[:, :], w_hi[par][:, part, col(k)], w_lo[par][:, part, col(k)],
                               hx_hi[:, k, ck(c)], hx_lo[:, k, ck(c)], k == 0, k == KH - 1)
                mm.then_inc(done, 1)

            def project_v(c, half):
                for t in range(2 * half, 2 * half + 2):
                    at = col(c * TPC + t)
                    for k in range(KH):
                        mm = three(pe, bank_v[:, col(t % 2, 2 * D)], hx_hi[:, k, at], hx_lo[:, k, at],
                                   v_hi[:, k, :], v_lo[:, k, :], k == 0, k == KH - 1)
                mm.then_inc(v_done, 1)

            def attend(u, v, par, c):
                pe.wait_ge(s_masked, u + 1)
                pe.wait_ge(v_sil, 2 * v)
                wait(pe, t1_done, u)
                wait(pe, sq_done, u)
                for t in range(TPC):
                    mm = pe.matmul(bank_o[:, col(t)], vt[:, c * TPC + t, col(par)], sm[:, col(t)],
                                   start=True, stop=True)
                mm.then_inc(o_done, 1)

            def project_out(u, par, n):
                g = 4 * u + n
                if n == 0:
                    pe.wait_ge(go_done, u + 1)
                if not isinstance(g, int) or g > 1:
                    pe.wait_ge(out_acc, g - 1)
                three(pe, bank_out[n % 2][:, :], w_hi[par][:, O, col(n)], w_lo[par][:, O, col(n)],
                      go_hi[:, :], go_lo[:, :], True, True).then_inc(out_done, 1)

            def unit(i, j):
                u, c, par, h, m = 8 * i + j, j % 4, j // 4 % 2, 2 * i + j // 4, i + j // 8
                bc, bpar, bh, bm = (j - 1) % 4, (j - 1) // 4 % 2, 2 * i + (j - 1) // 4, i + (j - 1) // 8
                if par == 0:
                    if c == 0:
                        pe.wait_ge(vl_done, 2 * m + 2)
                    wait(pe, v_sil, 8 * m + 2 * c)
                    project_v(c, 0)
                if c == 0:
                    pe.wait_ge(wl_done, 4 * h + 1)
                wait(pe, q_sil, u)
                project(par, Q, c, bank_q, q_done)
                if j > 0:
                    attend(u - 1, 4 * bm + 1 + bc if bpar == 0 else 4 * bm + 4, bpar, bc)
                if par == 0:
                    pe.wait_ge(v_sil, 8 * m + 2 * c + 1)
                    project_v(c, 1)
                if c == 0:
                    pe.wait_ge(wl_done, 4 * h + 2)
                wait(pe, k_sil, u)
                project(par, K, c, bank_k, k_done)
                if c == 0:
                    pe.wait_ge(wl_done, 4 * h + 3)
                wait(pe, g_tanh, u)
                project(par, G, c, bank_g, g_done)
                if j > 0:
                    if bc == 0:
                        pe.wait_ge(wl_done, 4 * bh + 4)
                    project_out(u - 1, bpar, 0)
                    project_out(u - 1, bpar, 1)
                pe.wait_ge(q_sil, u + 1)
                pe.wait_ge(k_sil, u + 1)
                wait(pe, s_masked, u)
                for t in range(TPC):
                    mm = pe.matmul(bank_s[:, col(t)], kt[:, col(t)], qt[:, col(t)], start=True, stop=True)
                mm.then_inc(s_done, 1)
                if j > 0:
                    project_out(u - 1, bpar, 2)
                    project_out(u - 1, bpar, 3)

            pe.wait_ge(mix_lo, NC * KH)
            unit(0, 0)
            unit(0, 1)
            with pe.Fori(0, HEADS // 2 - 1) as i:
                for j in range(2, 10):
                    unit(i, j)
            def sum_squares(c):
                pe.wait_ge(sq_added, LAST + c + 1)
                wait(pe, ms_done, c)
                pe.matmul(bank_v[:, :], ones[:, :], sq_acc[:, ck(c)], start=True, stop=True
                          ).then_inc(ss_done, 1)

            pe.wait_ge(ones_set, 1)
            for j in range(2, 8):
                unit(HEADS // 2 - 1, j)
                if j >= 5:
                    sum_squares(j - 5)
            attend(UNITS - 1, 4 * (HEADS // 2), 1, NC - 1)
            for n in range(4):
                project_out(UNITS - 1, 1, n)
            sum_squares(NC - 1)

            def transpose_a(g):
                pe.wait_ge(ld_ag[g % 2], 16 * (g // 2) + 16)
                wait(pe, at_copied, 2 * g)
                for m in range(2):
                    for k in range(KH):
                        mm = pe.transpose(banks[m][:, col(k)], ag[:, g % 2, col(KH * m + k)], ident[:, :])
                mm.then_inc(at_done, 1)

            pe.wait_ge(q_sil, UNITS)
            pe.wait_ge(k_sil, UNITS)
            pe.wait_ge(ld_late, 64)
            pe.wait_ge(go_done, UNITS)
            transpose_a(0)
            for g in range(NG):
                if g + 1 < NG:
                    transpose_a(g + 1)
                pe.wait_ge(at_copied, 2 * g + 2)
                pe.wait_ge(x1_done, g // GPC + 1)
                if g >= 2:
                    pe.wait_ge(rank_masked, g - 1)
                for m in range(2):
                    for k in range(KH):
                        mm = pe.matmul(banks[4 + g % 2][:, col(m, GT)], agt[:, g % 2, col(KH * m + k)],
                                       acc[:, k, col(g, GT)], start=(k == 0), stop=(k == KH - 1))
                mm.then_inc(rank_done, 1)

            def up_or_gate(par, part, c, dst, done):
                for k in range(KH):
                    at = slice(FW_AT[part] + k * P, FW_AT[part] + (k + 1) * P)
                    three(pe, dst[:, :], fw_hi[:, par, at], fw_lo[:, par, at],
                          hx_hi[:, k, ck(c)], hx_lo[:, k, ck(c)], k == 0, False)
                for g in range(GPC):
                    mm = pe.matmul(dst[:, col(g, GT)], fb[par][:, GPC * c + g, col(part)],
                                   lt[:, part, col(GPC * c + g, GT)], start=False, stop=(g == GPC - 1))
                mm.then_inc(done, 1)

            def funit(i, j, front=True):
                u, c, par, f = 8 * i + j, j % 4, j // 4 % 2, 2 * i + j // 4
                bpar, bf = (j - 1) // 4 % 2, 2 * i + (j - 1) // 4

                def downs(ns):
                    for n in ns:
                        g = FOUT * (u - 1) + n
                        if n == 0:
                            pe.wait_ge(fal_done, u)
                            if (j - 1) % 4 == 0:
                                pe.wait_ge(fl_done, 4 * bf + 4)
                        if not isinstance(g, int) or g > 3:
                            pe.wait_ge(f_acc, g - 3)
                        at = slice(FW_AT[2] + n * P, FW_AT[2] + (n + 1) * P)
                        three(pe, bank_f[(FOUT * (j - 1) + n) % 4][:, :], fw_hi[:, bpar, at],
                              fw_lo[:, bpar, at], fa_hi[:, :], fa_lo[:, :], True, True
                              ).then_inc(fo_done, 1)

                if front:
                    if c == 0:
                        pe.wait_ge(fl_done, 4 * f + 1)
                        pe.wait_ge(ld_fb[par], 16 * NG * (i + j // 8) + 16 * NG)
                    wait(pe, fg_sil, u)
                    up_or_gate(par, 0, c, bank_q, fg_done)
                if j > 0:
                    downs(range(3))
                if front:
                    if c == 0:
                        pe.wait_ge(fl_done, 4 * f + 2)
                    wait(pe, fact_done, u)
                    up_or_gate(par, 1, c, bank_k, fu_done)
                if j > 0:
                    downs(range(3, FOUT))

            pe.wait_ge(rank_masked, NG)
            pe.wait_ge(x1_lo, NC)
            funit(0, 0)
            funit(0, 1)
            with pe.Fori(0, FC // 2 - 1) as i:
                for j in range(2, 10):
                    funit(i, j)
            for j in range(2, 13):
                funit(FC // 2 - 1, j, front=j < 12)

            def bdown(c):
                pe.wait_ge(td_masked, c + 1)
                for o in range(KH):
                    n = KH * c + o
                    if n >= 4:
                        pe.wait_ge(y_done, n - 3)
                    for r in range(RK):
                        mm = pe.matmul(banks[n % 4][:, :], bdw[:, r, col(o)], td[:, r, ck(c)],
                                       start=(r == 0), stop=(r == RK - 1))
                    mm.then_inc(bd_done, 1)

            def linear(c):
                pe.wait_ge(yl_done, KH * (c + 1))
                for o in range(KH):
                    n = KH * c + o
                    if n >= 4:
                        pe.wait_ge(res_act, n - 3)
                    for k in range(KH):
                        pe.matmul(banks[4 + n % 4][:, :], sgn[:, k, col(o)], y_hi[:, c % 2, k, :],
                                  start=(k == 0), stop=False)
                        mm = pe.matmul(banks[4 + n % 4][:, :], sgn[:, k, col(o)], y_lo[:, c % 2, k, :],
                                       start=False, stop=(k == KH - 1))
                    mm.then_inc(lin_done, 1)

            pe.wait_ge(f_acc, FOUT * FUNITS)
            pe.wait_ge(ld_bd, 16)
            bdown(0)
            pe.wait_ge(abs_done, KH)
            for o in range(KH):
                for k in range(KH):
                    mm = pe.matmul(banks[4][:, o:o + 1], absw[:, k, col(o)], ones[:, 0:1],
                                   start=(k == 0), stop=(k == KH - 1))
            mm.then_inc(asum_done, 1)
            pe.wait_ge(alpha_done, 1)
            pe.wait_ge(sgn_done, KH)
            for c in range(NC):
                if c + 1 < NC:
                    bdown(c + 1)
                linear(c)

        @block.scalar
        def _(act):
            def head_hi(n, p, par):
                act.wait_ge(ld_w[p], 16 * n + 16)
                act.activation(w_hi[par][:, p, :], raw[:, p, :], ACT.Copy).then_inc(wh_done, 1)

            def v_hi_half(m, half):
                if half == 0:
                    act.wait_ge(ld_v, 16 * m + 16)
                at = slice(2 * half, 2 * half + 2)
                act.activation(v_hi[:, at, :], raw_v[:, at, :], ACT.Copy).then_inc(vh_done, 1)

            for n in range(NC * KH):
                c, k = n // KH, n % KH
                if n == 8:
                    v_hi_half(0, 0)
                    v_hi_half(0, 1)
                    for p in range(4):
                        head_hi(0, p, 0)
                act.wait_ge(mix_done, n + 1)
                act.activation(hx_hi[:, k, ck(c)], banks[n % 8][:, :], ACT.Copy).then_inc(mix_hi, 1)

            def silu_v(u_v, c, half):
                act.wait_ge(v_done, 2 * u_v + half + 1)
                act.activation(vt[:, c * TPC + 2 * half:c * TPC + 2 * half + 2, :],
                               bank_v[:, :].rearrange("p (t n) -> p t n", t=2), ACT.Silu).then_inc(v_sil, 1)

            def square(u):
                act.wait_ge(o_done, u + 1)
                wait(act, sq_added, u)
                act.activation(sq[:, :], bank_o[:, :], ACT.Square).then_inc(sq_done, 1)

            def unit(i, j, ahead=True):
                u, c, par, h, m = 8 * i + j, j % 4, j // 4 % 2, 2 * i + j // 4, i + j // 8
                if par == 0:
                    silu_v(4 * m + c, c, 0)
                act.wait_ge(q_done, u + 1)
                act.activation(qt[:, :], bank_q[:, :], ACT.Silu).then_inc(q_sil, 1)
                if j > 0:
                    square(u - 1)
                if ahead:
                    head_hi(h + 1, c, 1 - par)
                    if par == 1 and c < 2:
                        v_hi_half(m + 1, c)
                if par == 0:
                    silu_v(4 * m + c, c, 1)
                act.wait_ge(k_done, u + 1)
                act.activation(kt[:, :], bank_k[:, :], ACT.Silu).then_inc(k_sil, 1)
                act.wait_ge(g_done, u + 1)
                wait(act, t1_done, u)
                act.activation(tg[:, :], bank_g[:, :], ACT.Tanh, scale=0.5).then_inc(g_tanh, 1)

            unit(0, 0)
            unit(0, 1)
            with act.Fori(0, HEADS // 2 - 1) as i:
                for j in range(2, 10):
                    unit(i, j)
            def root(c):
                act.wait_ge(rec_done, c + 1)
                act.activation(sq_acc[:, ck(c)], sq_acc[:, ck(c)], ACT.Sqrt).then_inc(rstd_done, 1)

            def x1_his(c):
                act.wait_ge(x1_done, c + 1)
                act.activation(hx_hi[:, :, ck(c)], acc[:, :, ck(c)], ACT.Copy).then_inc(x1_hi, 1)

            def copy_at(g):
                act.wait_ge(at_done, g + 1)
                if g >= 2:
                    act.wait_ge(rank_done, g - 1)
                for m in range(2):
                    act.activation(agt[:, g % 2, col(m, HID)], banks[m][:, :], ACT.Copy
                                   ).then_inc(at_copied, 1)

            for j in range(2, 8):
                unit(HEADS // 2 - 1, j, ahead=j < 4)
                if j >= 6:
                    root(j - 6)
            square(UNITS - 1)
            x1_his(0)
            root(2)
            copy_at(0)
            copy_at(1)
            x1_his(1)
            root(3)
            for c in range(1, NC):
                copy_at(2 * c)
                copy_at(2 * c + 1)
                if c + 1 < NC:
                    x1_his(c + 1)

            def ffn_hi(f, p, par):
                act.wait_ge(ld_f[p], 16 * f + 16)
                at = slice(FW_AT[p], FW_AT[p + 1])
                act.activation(fw_hi[:, par, at], fraw[:, at], ACT.Copy).then_inc(fh_done, 1)

            def funit(i, j, ahead=True):
                u, c, par, f = 8 * i + j, j % 4, j // 4 % 2, 2 * i + j // 4
                act.wait_ge(fg_done, u + 1)
                wait(act, fact_done, u)
                act.activation(sg, bank_q[:, :], ACT.Silu).then_inc(fg_sil, 1)
                if ahead:
                    ffn_hi(f + 1, c, 1 - par)
                act.wait_ge(fact_done, u + 1)
                act.activation(fa_hi[:, :], ft, ACT.Copy).then_inc(fah_done, 1)

            for p in range(4):
                ffn_hi(0, p, 0)
            funit(0, 0)
            funit(0, 1)
            with act.Fori(0, FC // 2 - 1) as i:
                for j in range(2, 10):
                    funit(i, j)
            for j in range(2, 12):
                funit(FC // 2 - 1, j, ahead=j < 8)

            act.wait_ge(f_acc, FOUT * FUNITS)
            act.wait_ge(ld_lt, 16)
            for k in range(KH):
                act.activation(absw[:, k, :], lin_tt[:, k, :], ACT.Abs).then_inc(abs_done, 1)
            for k in range(KH):
                act.activation(sgn[:, k, :], lin_tt[:, k, :], ACT.Sign).then_inc(sgn_done, 1)

            def y_his(c):
                for o in range(KH):
                    n = KH * c + o
                    act.wait_ge(y_done, n + 1)
                    if c >= 2 and o == 0:
                        act.wait_ge(lin_done, KH * (c - 1))
                    act.activation(y_hi[:, c % 2, o, :], acc[:, o, ck(c)], ACT.Copy).then_inc(yh_done, 1)

            y_his(0)
            for c in range(NC):
                if c + 1 < NC:
                    y_his(c + 1)
                if c == 0:
                    act.wait_ge(alpha_done, 1)
                for o in range(KH):
                    n = KH * c + o
                    act.wait_ge(lin_done, n + 1)
                    if n >= 4:
                        act.wait_ge(stored[n % 4], 16 * (n // 4))
                    act.activation(res[:, n % 4, :], banks[4 + n % 4][:, :], ACT.Identity,
                                   scale=alpha[:, o:o + 1], bias=bias_sb[:, o:o + 1]).then_inc(res_act, 1)

        @block.vector
        def _(dve):
            dve.wait_ge(ld_small, 32)
            dve.tensor_scalar(gidx[:, :], cidx[:, :], float(SEQ), const[:, 0:1], ALU.mult, ALU.add
                              ).then_inc(idx_done, 1)
            dve.memset(mixw[:, :, :], 0.0).then_inc(mixw_zero, 1)

            def head_lo(n, p, par):
                dve.wait_ge(wh_done, 4 * n + p + 1)
                dve.tensor_tensor(w_lo[par][:, p, :], raw[:, p, :], w_hi[par][:, p, :].bitcast(F32),
                                  ALU.subtract).then_inc(wl_done, 1)

            def v_lo_half(m, half):
                dve.wait_ge(vh_done, 2 * m + half + 1)
                at = slice(2 * half, 2 * half + 2)
                dve.tensor_tensor(v_lo[:, at, :], raw_v[:, at, :], v_hi[:, at, :].bitcast(F32),
                                  ALU.subtract).then_inc(vl_done, 1)

            dve.wait_ge(mixw_zero, 1)
            for c in range(NC):
                ts = slice(c * TPC, (c + 1) * TPC)
                dve.wait_ge(ld_gath[c], 16 * TPC)
                for b in range(4):
                    rows = slice(SEQ * b, SEQ * (b + 1))
                    dve.tensor_copy(mixw[rows, ts, rows], gath[rows, ts, 0:SEQ]).then_inc(mixw_done, 1)
            for n in range(NC * KH):
                c, k = n // KH, n % KH
                if n == 8:
                    v_lo_half(0, 0)
                    v_lo_half(0, 1)
                    for p in range(4):
                        head_lo(0, p, 0)
                dve.wait_ge(mix_hi, n + 1)
                dve.tensor_tensor(hx_lo[:, k, ck(c)], banks[n % 8][:, :], hx_hi[:, k, ck(c)].bitcast(F32),
                                  ALU.subtract).then_inc(mix_lo, 1)

            dve.wait_ge(ld_late, 64)
            dve.tensor_scalar(aidx[:, :], ridx[:, :], float(RANK), const[:, 3:4], ALU.mult, ALU.add
                              ).then_inc(ridx_done, 1)
            dve.wait_ge(ridx_done, 1)
            for par in range(2):
                dve.tensor_scalar(fidx[:, par, :], aidx[:, :], float(par * CONDS * RANK), None, ALU.add
                                  ).then_inc(ridx_done, 1)
            dve.tensor_copy(lidxf[:, :], lidx[:, :]).then_inc(lidxf_done, 1)
            dve.wait_ge(lidxf_done, 1)
            for r in range(RK):
                dve.tensor_scalar(lmask[:, r, :], lidxf[:, :], const[:, 1 + r:2 + r], 0.5,
                                  ALU.is_equal, ALU.mult).then_inc(lmask_done, 1)

            def mask_s(u, par):
                dve.wait_ge(s_done, u + 1)
                dve.tensor_tensor(sm[:, :].rearrange("p (t n) -> p t n", t=TPC),
                                  bank_s[:, :].rearrange("p (t n) -> p t n", t=TPC),
                                  mb[:, par, 0:P].unsqueeze(1).to_broadcast([P, TPC, P]),
                                  ALU.mult).then_inc(s_masked, 1)

            def gate_o(u, par, c):
                dve.wait_ge(g_tanh, u + 1)
                dve.wait_ge(sq_done, u + 1)
                dve.scalar_tensor_tensor(out=t1[:, :], in0=tg[:, :], scalar=1.0, in1=bank_o[:, :],
                                         op0=ALU.add, op1=ALU.mult).then_inc(t1_done, 1)
                dve.wait_ge(t1_done, u + 1)
                dve.tensor_scalar(go_hi[:, :], t1[:, :], mb[:, par, P:P + 1], None, ALU.mult
                                  ).then_inc(goh_done, 1)
                dve.wait_ge(goh_done, u + 1)
                dve.scalar_tensor_tensor(out=go_lo[:, :], in0=t1[:, :], scalar=mb[:, par, P:P + 1],
                                         in1=go_hi[:, :].bitcast(F32), op0=ALU.mult, op1=ALU.subtract
                                         ).then_inc(go_done, 1)
                dve.tensor_tensor(sq_acc[:, ck(c)], sq_acc[:, ck(c)], sq[:, :], ALU.add
                                  ).then_inc(sq_added, 1)

            def add_out(u, c, n):
                dve.wait_ge(out_done, 4 * u + n + 1)
                dve.tensor_tensor(acc[:, n, ck(c)], acc[:, n, ck(c)], bank_out[n % 2][:, :], ALU.add
                                  ).then_inc(out_acc, 1)

            def unit(i, j, ahead=True):
                u, c, par, h, m = 8 * i + j, j % 4, j // 4 % 2, 2 * i + j // 4, i + j // 8
                bc, bpar = (j - 1) % 4, (j - 1) // 4 % 2
                if j > 0:
                    gate_o(u - 1, bpar, bc)
                if ahead:
                    head_lo(h + 1, c, 1 - par)
                    if par == 1 and c < 2:
                        v_lo_half(m + 1, c)
                if j > 0:
                    add_out(u - 1, bc, 0)
                    add_out(u - 1, bc, 1)
                if c == 0:
                    dve.wait_ge(ld_m[par], 16 * (i + j // 8) + 16)
                mask_s(u, par)
                if j > 0:
                    add_out(u - 1, bc, 2)
                    add_out(u - 1, bc, 3)

            dve.wait_ge(acc_zero, 2)
            unit(0, 0)
            unit(0, 1)
            with dve.Fori(0, HEADS // 2 - 1) as i:
                for j in range(2, 10):
                    unit(i, j)
            def mean(c):
                at = sq_acc[:, ck(c)]
                dve.wait_ge(ss_done, c + 1)
                dve.tensor_scalar(at, bank_v[:, :], 4.0 / HD, EPS, ALU.mult, ALU.add).then_inc(ms_done, 1)
                dve.wait_ge(ms_done, c + 1)
                dve.reciprocal(at, at).then_inc(rec_done, 1)

            def norm(c):
                at = acc[:, :, ck(c)]
                dve.wait_ge(rstd_done, c + 1)
                dve.tensor_tensor(at, at, sq_acc[:, ck(c)].unsqueeze(1).to_broadcast([P, KH, NT]),
                                  ALU.mult).then_inc(nrm_done, 1)
                dve.wait_ge(nrm_done, c + 1)
                dve.wait_ge(ld_xt[c], 16)
                dve.tensor_tensor(at, at, lt[:, :, ck(c)], ALU.add).then_inc(x1_done, 1)

            def mask_ranks(g):
                dve.wait_ge(rank_done, g + 1)
                dve.tensor_tensor(lt[:, 0:2, col(g, GT)].rearrange("p m (b s) -> p m b s", s=SEQ),
                                  banks[4 + g % 2][:, :].rearrange("p (m b s) -> p m b s", m=2, s=SEQ),
                                  const[:, 4:4 + GB].unsqueeze(1).unsqueeze(3).to_broadcast([P, 2, GB, SEQ]),
                                  ALU.mult).then_inc(rank_masked, 1)

            for j in range(2, 8):
                unit(HEADS // 2 - 1, j, ahead=j < 4)
                if j >= 5:
                    mean(j - 5)
                if j >= 7:
                    norm(j - 7)
            gate_o(UNITS - 1, 1, NC - 1)
            for n in range(4):
                add_out(UNITS - 1, NC - 1, n)
            mean(NC - 1)
            norm(1)
            for c in range(NC):
                mask_ranks(GPC * c)
                mask_ranks(GPC * c + 1)
                if c + 2 < NC:
                    norm(c + 2)

            def ffn_lo(f, p, par):
                dve.wait_ge(fh_done, 4 * f + p + 1)
                at = slice(FW_AT[p], FW_AT[p + 1])
                dve.tensor_tensor(fw_lo[:, par, at], fraw[:, at], fw_hi[:, par, at].bitcast(F32),
                                  ALU.subtract).then_inc(fl_done, 1)

            def add_down(u, j, n):
                c = j % 4
                dve.wait_ge(fo_done, FOUT * u + n + 1)
                dst = acc[:, n, ck(c)] if n < KH else td[:, n - KH, ck(c)]
                dve.tensor_tensor(dst, dst, bank_f[(FOUT * j + n) % 4][:, :], ALU.add).then_inc(f_acc, 1)

            def funit(i, j, front=True, ahead=True):
                u, c, par, f = 8 * i + j, j % 4, j // 4 % 2, 2 * i + j // 4
                if j > 0:
                    for n in range(3):
                        add_down(u - 1, j - 1, n)
                if ahead:
                    ffn_lo(f + 1, c, 1 - par)
                if j > 0:
                    for n in range(3, FOUT):
                        add_down(u - 1, j - 1, n)
                if front:
                    dve.wait_ge(fu_done, u + 1)
                    dve.wait_ge(fg_sil, u + 1)
                    dve.tensor_tensor(ft, sg, bank_k[:, :], ALU.mult).then_inc(fact_done, 1)
                    dve.wait_ge(fah_done, u + 1)
                    dve.tensor_tensor(fa_lo[:, :], ft, fa_hi[:, :].bitcast(F32), ALU.subtract
                                      ).then_inc(fal_done, 1)

            for p in range(4):
                ffn_lo(0, p, 0)
            funit(0, 0)
            dve.wait_ge(facc_zero, 1 + NC)
            funit(0, 1)
            with dve.Fori(0, FC // 2 - 1) as i:
                for j in range(2, 10):
                    funit(i, j)
            for j in range(2, 13):
                funit(FC // 2 - 1, j, front=j < 12, ahead=j < 8)

            dve.wait_ge(lmask_done, RK)
            for c in range(NC):
                for r in range(RK):
                    at = td[:, r, ck(c)].rearrange("p (b s) -> p b s", s=SEQ)
                    half = lmask[:, r, c * BPC:(c + 1) * BPC].unsqueeze(2).to_broadcast([P, BPC, SEQ])
                    m = dve.tensor_tensor(at, at, half, ALU.mult)
                m.then_inc(td_masked, 1)
                if c == 0:
                    dve.wait_ge(asum_done, 1)
                    dve.tensor_scalar(alpha[:, :], banks[4][:, 0:KH], 1.0 / HID, None, ALU.mult
                                      ).then_inc(alpha_done, 1)

            def y_los(c):
                for o in range(KH):
                    n = KH * c + o
                    dve.wait_ge(bd_done, n + 1)
                    dve.tensor_tensor(acc[:, o, ck(c)], acc[:, o, ck(c)], banks[n % 4][:, :], ALU.add
                                      ).then_inc(y_done, 1)
                for o in range(KH):
                    n = KH * c + o
                    dve.wait_ge(yh_done, n + 1)
                    dve.tensor_tensor(y_lo[:, c % 2, o, :], acc[:, o, ck(c)],
                                      y_hi[:, c % 2, o, :].bitcast(F32), ALU.subtract).then_inc(yl_done, 1)

            y_los(0)
            for c in range(NC):
                if c + 1 < NC:
                    y_los(c + 1)
                for o in range(KH):
                    n = KH * c + o
                    r = res[:, n % 4, :]
                    dve.wait_ge(res_act, n + 1)
                    dve.tensor_tensor(r, r, hx_hi[:, o, ck(c)].bitcast(F32), ALU.add).then_inc(res_a, 1)
                    dve.wait_ge(res_a, n + 1)
                    dve.tensor_tensor(r, r, hx_lo[:, o, ck(c)].bitcast(F32), ALU.add).then_inc(res_done, 1)


def decay_masks():
    layer, layers = 1, 32
    base = np.float32(1.0 / 2.0 ** (8.0 / HEADS))
    factor = np.float32(1.0 - layer / (layers - 1 + 1e-05) + 1e-05)
    slope = base ** (np.arange(HEADS, dtype=np.float32) + 1) * factor
    diff = np.arange(SEQ)[None, :] - np.arange(SEQ)[:, None]
    one = np.where(diff >= 0, np.exp(-slope[:, None, None] * np.maximum(diff, 0)), 0.0) * 0.5
    full = np.zeros((HEADS, P, P), np.float32)
    for b in range(P // SEQ):
        full[:, b * SEQ:(b + 1) * SEQ, b * SEQ:(b + 1) * SEQ] = one
    return full


def kernel(**inputs):
    import concourse.bacc as bacc
    from concourse.bass_utils import run_bass_kernel_spmd

    x = np.asarray(inputs["x"])
    cond = np.asarray(inputs["itok_B_0_15"]).astype(np.int32)
    lora = np.asarray(inputs["itok_B_2_6"]).astype(np.int32)

    def chunked(w):
        return np.asarray(w).reshape(-1, KH, P).transpose(2, 1, 0)

    qkv = np.asarray(inputs["L0_attn_qkv_w"]).reshape(HEADS, 3, D, KH, P)
    by_head = qkv.transpose(0, 1, 4, 3, 2)
    gate = np.asarray(inputs["L0_attn_gate_w"]).reshape(HEADS, D, KH, P).transpose(0, 3, 2, 1)
    outw = np.asarray(inputs["L0_attn_out_w"]).reshape(HID, HEADS, D).transpose(1, 2, 0)
    head_w = np.stack([by_head[:, 0].reshape(HEADS, P, HID), by_head[:, 1].reshape(HEADS, P, HID),
                       gate.reshape(HEADS, P, HID), outw], 1)
    v_w = by_head[:, 2].reshape(HEADS // 2, 2, P, KH, D).transpose(0, 2, 3, 1, 4).reshape(
        HEADS // 2, P, KH, 2 * D)
    norm = np.asarray(inputs["L0_attn_norm_w"]).reshape(HEADS, D, 1)
    misc = np.concatenate([decay_masks(), norm], 2)

    def padded(w, axis):
        shape = list(w.shape)
        shape[axis] = FC * P - F
        return np.concatenate([w, np.zeros(shape, w.dtype)], axis)

    def hidden(w):
        return padded(np.asarray(w), 0).reshape(FC, P, KH, P).transpose(0, 3, 2, 1).reshape(FC, P, HID)

    downw = padded(np.asarray(inputs["L0_cond2_W_down"]), 1).reshape(HID, FC, P).transpose(1, 2, 0)
    adown = padded(np.asarray(inputs["L0_cond2_A_down"])[0], 2).reshape(CONDS * RANK, FC, P).transpose(1, 2, 0)
    ffn_w = np.concatenate([hidden(inputs["L0_cond2_W_gate"]), hidden(inputs["L0_cond2_W_up"]),
                            downw, adown], 2)

    def ranks(w):
        w = padded(np.asarray(w)[0], 1).transpose(0, 2, 1).reshape(CONDS * RANK, FC, P)
        return w.transpose(1, 0, 2).reshape(FC * CONDS * RANK, P)

    b_w = np.concatenate([ranks(inputs["L0_cond2_B_gate"]), ranks(inputs["L0_cond2_B_up"])], 1)
    a_w = np.concatenate([np.asarray(inputs[n])[0].reshape(CONDS * RANK, HID)
                          for n in ("L0_cond2_A_gate", "L0_cond2_A_up")], 1)
    bdown = np.asarray(inputs["L0_cond2_B_down"])[0].transpose(0, 2, 1).reshape(RK, P, HID).transpose(1, 0, 2)
    lin = np.asarray(inputs["L0_ffn_weight_real"])
    rows = np.arange(P)
    consts = np.stack([rows % SEQ, rows // RANK, rows // RANK + P // RANK, rows % RANK]
                      + [0.5 * (rows // RANK == j) for j in range(GB)], 1).astype(np.float32)
    arrays = dict(
        x_tok=x.reshape(TILES, P, HID).transpose(1, 0, 2),
        x_t=chunked(x.reshape(TOK, HID)),
        cond_idx=np.repeat(cond.reshape(TILES, 4).T, SEQ, 0),
        lora_idx=np.repeat(lora.reshape(1, BATCH), P, 0),
        rank_idx=np.repeat(lora.reshape(NG, GB).T, RANK, 0),
        consts=consts, eye=np.eye(P, dtype=np.float32),
        cond_w=np.asarray(inputs["L0_cond_weights"]).reshape(CONDS * SEQ, SEQ),
        head_w=head_w, v_w=v_w, misc=misc, a_w=a_w, ffn_w=ffn_w, b_w=b_w, bdown_w=bdown,
        lin_t=chunked(lin),
        bias=np.asarray(inputs["L0_ffn_bias"]).reshape(KH, P).T,
    )
    arrays = {n: np.ascontiguousarray(a) for n, a in arrays.items()}
    nc = bacc.Bacc("TRN2", target_bir_lowering=False, num_devices=1)
    args = {n: nc.dram_tensor(n + "_dram", a.shape, mybir.dt.from_np(a.dtype), kind="ExternalInput").ap()
            for n, a in arrays.items()}
    out = nc.dram_tensor("out_dram", (KH, P, TOK), F32, kind="ExternalOutput").ap()
    build(nc, *args.values(), out)
    r = run_bass_kernel_spmd(nc, [{n + "_dram": a for n, a in arrays.items()}], core_ids=[0])
    got = np.asarray(r.results[0]["out_dram"])
    return got.reshape(HID, TOK).T.reshape(BATCH, SEQ, HID)
```

```python
from contextlib import ExitStack

import numpy as np

import concourse.bass as bass
from concourse import mybir

F32 = mybir.dt.float32
F32R = mybir.dt.float32r
I32 = mybir.dt.int32
U32 = mybir.dt.uint32
ALU = mybir.AluOpType
ACT = mybir.ActivationFunctionType

P = 128
BATCH, SEQ, HID = 64, 32, 512
TOK = BATCH * SEQ
KH = HID // P
NT = 512
NC = TOK // NT
TILES = TOK // P
TPC = NT // P
HEADS, D = 32, 128
CONDS, RANK = 16, 16
F = 1376
FC = -(-F // P)
EPS = 1e-5
HD = HEADS * D
UNITS = HEADS * NC
FUNITS = FC * NC
Q, K, G, O = range(4)
GB = P // RANK
GT = GB * SEQ
NG = TOK // GT
GPC = NT // GT
LAST = UNITS - NC
FW_AT = [0, HID, 2 * HID, 3 * HID]
FP = len(FW_AT) - 1


def wait(eng, sem, value):
    if not isinstance(value, int) or value > 0:
        eng.wait_ge(sem, value)


def ck(c):
    return slice(c * NT, (c + 1) * NT)


def col(n, w=P):
    return slice(n * w, (n + 1) * w)


def build(nc, x_tok, x_t, cond_idx, rank_idx, consts, eye, cond_w, head_w, v_w, misc, a_w,
          ffn_w, b_w, bdown_w, lin_n, lin_t, bias, out):
    with ExitStack() as ctx:
        def sem(name):
            return ctx.enter_context(nc.semaphore(name))

        def sb(name, shape, dt=F32, scope=ctx):
            return scope.enter_context(nc.sbuf_tensor(name, shape, dt))

        banks = [ctx.enter_context(nc.psum_tensor(f"bank{n}", [P, NT], F32)) for n in range(8)]
        bank_q, bank_k, bank_g, bank_v, bank_s, bank_o, bank_x0, bank_x1 = banks
        bank_out = [bank_x0, bank_x1]
        bank_rank = [bank_s, bank_g]
        bank_f = [bank_s, bank_o, bank_x0, bank_x1]
        bank_bd = [bank_v, bank_q, bank_k]

        acc = sb("acc", [P, KH, TOK])
        hx_hi = sb("hx_hi", [P, KH, TOK], F32R)
        hx_lo = sb("hx_lo", [P, KH, TOK], F32R)
        sq_acc = sb("sq_acc", [P, TOK])
        const = sb("const", [P, 2 + GB])
        cidx = sb("cidx", [P, TILES], I32)
        ridx = sb("ridx", [P, NG], I32)
        fidx = sb("fidx", [P, 2, NG], U32)
        fstep = sb("fstep", [P, NG], U32)
        aidx = sb("aidx", [P, NG], U32)
        ones = sb("ones", [P, P])
        ident = sb("ident", [P, P])
        bias_sb = sb("bias_sb", [P, KH])
        alpha = sb("alpha", [P, KH])

        att = ExitStack()
        v_hi = sb("v_hi", [P, KH, 2 * D], F32R, att)
        v_lo = sb("v_lo", [P, KH, 2 * D], F32R, att)
        raw_v = sb("raw_v", [P, KH, 2 * D], F32, att)
        raw = sb("raw", [P, 4, HID], F32, att)
        w_hi, w_lo = [None, None], [None, None]
        w_hi[0] = sb("w_hi0", [P, 4, HID], F32R, att)
        w_lo[0] = sb("w_lo0", [P, 4, HID], F32R, att)
        mixw = sb("mixw", [P, TILES, P], F32, att)
        gath = sb("gath", [P, TILES, SEQ], F32, att)
        sm = sb("sm", [P, NT], F32, att)
        w_hi[1] = sb("w_hi1", [P, 4, HID], F32R, att)
        w_lo[1] = sb("w_lo1", [P, 4, HID], F32R, att)
        mb = sb("mb", [P, 2, P + 1], F32, att)
        qt = sb("qt", [P, NT], F32, att)
        kt = sb("kt", [P, NT], F32, att)
        vt = sb("vt", [P, TILES, 2 * D], F32, att)
        tg = sb("tg", [P, NT], F32, att)
        sq = sb("sq", [P, NT], F32, att)
        t1 = sb("t1", [P, NT], F32, att)
        go_hi = sb("go_hi", [P, NT], F32R, att)
        go_lo = sb("go_lo", [P, NT], F32R, att)
        gidx = sb("gidx", [P, TILES], U32, att)
        att.close()

        norm_stage = ExitStack()
        lt = sb("lt", [P, NC, TOK], F32, norm_stage)
        rk = lt[:, 0:2, :]
        ag01 = sb("ag01", [P, 2, 2 * HID], F32, norm_stage)
        ag = [ag01[:, 0, :], ag01[:, 1, :], lt[:, 3, 0:2 * HID], lt[:, 3, 2 * HID:4 * HID]]
        agt = sb("agt", [P, 2, 2 * HID], F32, norm_stage)
        x3 = sb("x3", [P, TOK], F32, norm_stage)
        x_at = [lt[:, 0, :], lt[:, 1, :], lt[:, 2, :], x3[:, :]]
        x_c = [x_at[c].rearrange("p (k n) -> p k n", k=KH) for c in range(NC)]
        norm_stage.close()

        rk_lo = sb("rk_lo", [P, 2, TOK], F32R)
        rk_hi = sb("rk_hi", [P, 2, TOK], F32R)
        td = sb("td", [P, TOK])
        bdg = [sb(f"bdg{n}", [P, GPC, HID]) for n in range(2)]
        ffn = ExitStack()
        fw_hi, fw_lo = [None, None], [None, None]
        for par in (1, 0):
            fw_hi[par] = sb(f"fw_hi{par}", [P, FW_AT[-1]], F32R, ffn)
            fw_lo[par] = sb(f"fw_lo{par}", [P, FW_AT[-1]], F32R, ffn)
            if par == 1:
                fraw = sb("fraw", [P, FW_AT[-1]], F32, ffn)
                fa_hi = sb("fa_hi", [P, NT], F32R, ffn)
                fa_lo = sb("fa_lo", [P, NT], F32R, ffn)
        lraw = sb("lraw", [P, 2, GPC, 3 * P], F32, ffn)
        lb_hi = sb("lb_hi", [P, 2, GPC, 2 * P], F32R, ffn)
        lb_lo = sb("lb_lo", [P, 2, GPC, 2 * P], F32R, ffn)
        la_hi = sb("la_hi", [P, 2, GPC * P], F32R, ffn)
        la_lo = sb("la_lo", [P, 2, GPC * P], F32R, ffn)
        sg = sq_acc[:, 0:NT]
        ft = sq_acc[:, NT:2 * NT]
        ffn.close()

        lin_stage = ExitStack()
        lin_tt = sb("lin_tt", [P, KH, HID], F32, lin_stage)
        lin_stage.close()
        sgn = sb("sgn", [P, KH, HID], F32R)
        bdg.append(sb("bdg2", [P, GPC, HID]))
        res = sb("res", [P, 4, NT])
        y_lo = rk_lo[:, :, :].rearrange("p a (o n) -> p a o n", o=KH)
        y_hi = rk_hi[:, :, :].rearrange("p a (o n) -> p a o n", o=KH)
        lin_rows = [fraw[:, col(k, HID)] for k in range(KH - 1)] + [sq_acc[:, 2 * NT:2 * NT + HID]]

        ld_small, ones_set, ld_late = sem("ld_small"), sem("ones_set"), sem("ld_late")
        ld_gath = [sem(f"ld_gath{c}") for c in range(NC)]
        ld_x = [sem(f"ld_x{c}") for c in range(NC)]
        ld_w = [sem(f"ld_w{p}") for p in range(4)]
        ld_v = sem("ld_v")
        ld_m = [sem(f"ld_m{p}") for p in range(2)]
        idx_done, mixw_zero, mixw_done = sem("idx_done"), sem("mixw_zero"), sem("mixw_done")
        mix_done, mix_hi, mix_lo = sem("mix_done"), sem("mix_hi"), sem("mix_lo")
        acc_zero = sem("acc_zero")
        wh_done, wl_done, vh_done, vl_done = sem("wh_done"), sem("wl_done"), sem("vh_done"), sem("vl_done")
        q_done, k_done, g_done, v_done = sem("q_done"), sem("k_done"), sem("g_done"), sem("v_done")
        s_done, o_done, out_done = sem("s_done"), sem("o_done"), sem("out_done")
        q_sil, k_sil, v_sil, g_tanh, sq_done = sem("q_sil"), sem("k_sil"), sem("v_sil"), sem("g_tanh"), sem("sq_done")
        s_masked, t1_done, goh_done, go_done = sem("s_masked"), sem("t1_done"), sem("goh_done"), sem("go_done")
        sq_added, out_acc = sem("sq_added"), sem("out_acc")
        ld_xt = [sem(f"ld_xt{c}") for c in range(NC)]
        ld_ag = [sem(f"ld_ag{n}") for n in range(4)]
        ridx_done, rk_hi_done, rk_lo_done = sem("ridx_done"), sem("rk_hi_done"), sem("rk_lo_done")
        fidx_done, fidx_seen, at_done, at_copied = sem("fidx_done"), sem("fidx_seen"), sem("at_done"), sem("at_copied")
        ss_done, ms_done, rec_done, rstd_done = sem("ss_done"), sem("ms_done"), sem("rec_done"), sem("rstd_done")
        nrm_done, x1_done, x1_hi, x1_lo = sem("nrm_done"), sem("x1_done"), sem("x1_hi"), sem("x1_lo")
        rank_done, rank_masked, facc_zero = sem("rank_done"), sem("rank_masked"), sem("facc_zero")
        ld_f = [sem(f"ld_f{p}") for p in range(FP)]
        ld_lw = [sem(f"ld_lw{p}") for p in range(2)]
        lbh_done, lbl_done, lah_done, lal_done = sem("lbh_done"), sem("lbl_done"), sem("lah_done"), sem("lal_done")
        la_done, td_done, td_acc = sem("la_done"), sem("td_done"), sem("td_acc")
        fh_done, fl_done = sem("fh_done"), sem("fl_done")
        fg_done, fu_done, fo_done = sem("fg_done"), sem("fu_done"), sem("fo_done")
        fg_sil, fact_done, fah_done, fal_done, f_acc = sem("fg_sil"), sem("fact_done"), sem("fah_done"), sem("fal_done"), sem("f_acc")
        ld_bd = [sem(f"ld_bd{n}") for n in range(3)]
        ld_ln, ld_lt, sgn_done, alpha_done = sem("ld_ln"), sem("ld_lt"), sem("sgn_done"), sem("alpha_done")
        td_masked, bd_done, y_done, yh_done, yl0_done, yl_done = sem("td_masked"), sem("bd_done"), sem("y_done"), sem("yh_done"), sem("yl0_done"), sem("yl_done")
        lin_done, res_act, res_a, res_done = sem("lin_done"), sem("res_act"), sem("res_a"), sem("res_done")
        stored = [sem(f"stored{r}") for r in range(4)]

        def bank_mix(n):
            return banks[n] if n < KH else [bank_o, bank_x0, bank_x1][(n - KH) % 3]

        x_tiles = acc[:, :, :].rearrange("p k (a n) -> p (k a) n", n=HID)

        def three(pe, dst, w_h, w_l, x_h, x_l, first, last):
            pe.matmul(dst, w_h, x_h, start=first, stop=False)
            pe.matmul(dst, w_h, x_l, start=False, stop=False)
            return pe.matmul(dst, w_l, x_h, start=False, stop=last)

        block = ctx.enter_context(nc.Block())

        @block.sync
        def _(sp):
            sp.dma_start(cidx[:, :], cond_idx).then_inc(ld_small, 16)
            sp.dma_start(const[:, :], consts).then_inc(ld_small, 16)

            def load_x(c):
                at = slice(c * TPC, (c + 1) * TPC)
                sp.dma_start(x_tiles[:, at, :], x_tok[:, at, :]).then_inc(ld_x[c], 16)

            load_x(0)
            sp.wait_ge(ld_gath[0], 16 * TPC)
            sp.dma_start(raw_v[:, :, :], v_w[0]).then_inc(ld_v, 16)
            for p in range(4):
                sp.dma_start(raw[:, p, :], head_w[0, p]).then_inc(ld_w[p], 16)
            load_x(1)
            load_x(2)
            load_x(3)
            sp.dma_start(ridx[:, :], rank_idx).then_inc(ld_late, 16)
            sp.dma_start(bias_sb[:, :], bias).then_inc(ld_late, 16)
            sp.dma_start(ident[:, :], eye).then_inc(ld_late, 16)

            def load_head(n):
                for p in range(4):
                    sp.wait_ge(wl_done, 4 * n + p - 3)
                    sp.dma_start(raw[:, p, :], head_w[bass.ds(n, 1), p].rearrange("a p n -> p (a n)")
                                 ).then_inc(ld_w[p], 16)

            load_head(1)
            with sp.Fori(1, HEADS // 2) as m:
                sp.wait_ge(vl_done, 2 * m)
                sp.dma_start(raw_v[:, :, :], v_w[bass.ds(m, 1)].rearrange("a p k n -> p (a k) n")
                             ).then_inc(ld_v, 16)
                load_head(2 * m)
                load_head(2 * m + 1)

            sp.wait_ge(out_acc, 4 * LAST)
            for c in range(NC):
                if c == NC - 1:
                    sp.wait_ge(out_acc, 4 * UNITS)
                sp.dma_start(x_at[c], x_t[:, c, :]).then_inc(ld_xt[c], 16)
            for p in range(FP):
                sp.dma_start(fraw[:, FW_AT[p]:FW_AT[p + 1]], ffn_w[0, :, FW_AT[p]:FW_AT[p + 1]]
                             ).then_inc(ld_f[p], 16)
            with sp.Fori(1, FC) as f:
                for p in range(FP):
                    sp.wait_ge(fl_done, FP * f + p - FP + 1)
                    sp.dma_start(fraw[:, FW_AT[p]:FW_AT[p + 1]],
                                 ffn_w[bass.ds(f, 1), :, FW_AT[p]:FW_AT[p + 1]].rearrange("a p n -> p (a n)")
                                 ).then_inc(ld_f[p], 16)
            sp.wait_ge(fl_done, FP * FC)
            for o in range(KH):
                sp.dma_start(lin_rows[o], lin_n[o]).then_inc(ld_ln, 16)
            sp.wait_ge(fo_done, KH * (FUNITS - NC))
            sp.dma_start(lin_tt[:, :, :], lin_t).then_inc(ld_lt, 16)

            for n in range(NC * KH):
                c, o = n // KH, n % KH
                sp.wait_ge(res_done, n + 1)
                sp.dma_start(out[o, :, ck(c)], res[:, n % 4, :]).then_inc(stored[n % 4], 16)
            for r in range(4):
                sp.wait_ge(stored[r], 16 * NC * KH // 4)

        @block.gpsimd
        def _(pool):
            pool.wait_ge(idx_done, 1)
            for t in range(TILES):
                pool.indirect_dma_start(gath[:, t, :], None, cond_w,
                                        bass.IndirectOffsetOnAxis(ap=gidx[:, t:t + 1], axis=0)
                                        ).then_inc(ld_gath[t // TPC], 16)
            pool.memset(ones[:, :], 1.0).then_inc(ones_set, 1)
            pool.memset(sq_acc[:, :], 0.0).then_inc(acc_zero, 1)

            def load_misc(n, par):
                pool.dma_start(mb[:, par, :], misc[bass.ds(n, 1)].rearrange("a p n -> p (a n)")
                               ).then_inc(ld_m[par], 16)

            load_misc(0, 0)
            load_misc(1, 1)
            pool.wait_ge(mix_done, NC * KH)
            for c in range(NC):
                pool.memset(acc[:, :, ck(c)], 0.0).then_inc(acc_zero, 1)
            with pool.Fori(1, HEADS // 2) as m:
                for par in range(2):
                    pool.wait_ge(go_done, 8 * m - 4 + 4 * par)
                    load_misc(2 * m + par, par)

            def gather_a(g):
                if g >= 4:
                    pool.wait_ge(at_done, g - 3)
                pool.indirect_dma_start(ag[g % 4], None, a_w,
                                        bass.IndirectOffsetOnAxis(ap=aidx[:, g:g + 1], axis=0)
                                        ).then_inc(ld_ag[g % 4], 16)

            def gather_lora(slot, par, c):
                for g in range(GPC):
                    n = GPC * c + g
                    pool.indirect_dma_start(lraw[:, slot, g, :], None, b_w,
                                            bass.IndirectOffsetOnAxis(ap=fidx[:, par, n:n + 1], axis=0)
                                            ).then_inc(ld_lw[slot], 16)

            def gather_bdown(c):
                for g in range(GPC):
                    n = GPC * c + g
                    pool.indirect_dma_start(bdg[c % 3][:, g, :], None, bdown_w,
                                            bass.IndirectOffsetOnAxis(ap=aidx[:, n:n + 1], axis=0)
                                            ).then_inc(ld_bd[c % 3], 16)

            def split_x1(c):
                pool.wait_ge(x1_hi, c + 1)
                pool.tensor_tensor(hx_lo[:, :, ck(c)], acc[:, :, ck(c)], hx_hi[:, :, ck(c)].bitcast(F32),
                                   ALU.subtract).then_inc(x1_lo, 1)

            pool.wait_ge(ridx_done, 3)
            pool.wait_ge(out_acc, 4 * LAST)
            pool.memset(fstep[:, :], 2 * CONDS * RANK).then_inc(fidx_done, 1)
            for g in range(4):
                gather_a(g)
            for c in range(NC):
                if c == NC - 1:
                    pool.wait_ge(out_acc, 4 * UNITS)
                    gather_lora(0, 0, 0)
                    gather_lora(1, 0, 1)
                split_x1(c)
                if c < 2:
                    gather_a(2 * c + 4)
                    gather_a(2 * c + 5)
            pool.wait_ge(x1_lo, NC)
            for c in range(NC):
                pool.wait_ge(rank_done, GPC * (c + 1))
                pool.memset(acc[:, :, ck(c)], 0.0).then_inc(facc_zero, 1)
            pool.memset(td[:, :], 0.0).then_inc(facc_zero, 1)

            def next_lora(m, j):
                u, c, par, f = 8 * m + j, j % 4, j // 4 % 2, 2 * m + j // 4
                pool.wait_ge(lbl_done, u - 1)
                pool.wait_ge(la_done, u - 1)
                if c == 0 and not (isinstance(f, int) and f < 2):
                    pool.tensor_tensor(fidx[:, par, :], fidx[:, par, :], fstep[:, :], ALU.add
                                       ).then_inc(fidx_done, 1)
                    pool.wait_ge(fidx_done, f)
                pool.sem_inc(fidx_seen, 1)
                gather_lora(j % 2, par, c)

            pool.wait_ge(fidx_done, 1)
            for j in range(2, 8):
                next_lora(0, j)
            gather_bdown(0)
            gather_bdown(1)
            with pool.Fori(1, FUNITS // 8) as m:
                for j in range(8):
                    next_lora(m, j)
            for j in range(FUNITS % 8):
                next_lora(FUNITS // 8, j)
            pool.wait_ge(fo_done, KH * (FUNITS - NC))
            gather_bdown(2)
            pool.wait_ge(bd_done, KH)
            gather_bdown(3)
            for o in range(KH):
                pool.wait_ge(yh_done, o + 1)
                pool.tensor_tensor(y_lo[:, 0, o, :], acc[:, o, ck(0)], y_hi[:, 0, o, :].bitcast(F32),
                                   ALU.subtract).then_inc(yl0_done, 1)

        @block.tensor
        def _(pe):
            def mix(c):
                pe.wait_ge(ld_x[c], 16)
                pe.wait_ge(mixw_done, 4 * (c + 1))
                for k in range(KH):
                    n = KH * c + k
                    if n > KH + 2:
                        pe.wait_ge(mix_lo, n - 2)
                    for t in range(TPC):
                        mm = pe.matmul(bank_mix(n)[:, col(t)], x_tiles[:, c * TPC + t, col(k)],
                                       mixw[:, c * TPC + t, :], start=True, stop=True)
                    mm.then_inc(mix_done, 1)

            def project(par, part, c, dst, done):
                for k in range(KH):
                    mm = three(pe, dst[:, :], w_hi[par][:, part, col(k)], w_lo[par][:, part, col(k)],
                               hx_hi[:, k, ck(c)], hx_lo[:, k, ck(c)], k == 0, k == KH - 1)
                mm.then_inc(done, 1)

            def project_v(c, half):
                for t in range(2 * half, 2 * half + 2):
                    at = col(c * TPC + t)
                    for k in range(KH):
                        mm = three(pe, bank_v[:, col(t % 2, 2 * D)], hx_hi[:, k, at], hx_lo[:, k, at],
                                   v_hi[:, k, :], v_lo[:, k, :], k == 0, k == KH - 1)
                mm.then_inc(v_done, 1)

            def attend(u, v, par, c):
                pe.wait_ge(s_masked, u + 1)
                pe.wait_ge(v_sil, 2 * v)
                wait(pe, t1_done, u)
                wait(pe, sq_done, u)
                for t in range(TPC):
                    mm = pe.matmul(bank_o[:, col(t)], vt[:, c * TPC + t, col(par)], sm[:, col(t)],
                                   start=True, stop=True)
                mm.then_inc(o_done, 1)

            def project_out(u, par, n):
                g = 4 * u + n
                if n == 0:
                    pe.wait_ge(go_done, u + 1)
                if not isinstance(g, int) or g > 1:
                    pe.wait_ge(out_acc, g - 1)
                three(pe, bank_out[n % 2][:, :], w_hi[par][:, O, col(n)], w_lo[par][:, O, col(n)],
                      go_hi[:, :], go_lo[:, :], True, True).then_inc(out_done, 1)

            def unit(i, j, mixing=False):
                u, c, par, h, m = 8 * i + j, j % 4, j // 4 % 2, 2 * i + j // 4, i + j // 8
                bc, bpar, bh, bm = (j - 1) % 4, (j - 1) // 4 % 2, 2 * i + (j - 1) // 4, i + (j - 1) // 8
                if par == 0:
                    if c == 0:
                        pe.wait_ge(vl_done, 2 * m + 2)
                    wait(pe, v_sil, 8 * m + 2 * c)
                    project_v(c, 0)
                if c == 0:
                    pe.wait_ge(wl_done, 4 * h + 1)
                wait(pe, q_sil, u)
                project(par, Q, c, bank_q, q_done)
                if mixing:
                    pe.wait_ge(mix_lo, NC * KH)
                if j > 0:
                    attend(u - 1, 4 * bm + 1 + bc if bpar == 0 else 4 * bm + 4, bpar, bc)
                if par == 0:
                    pe.wait_ge(v_sil, 8 * m + 2 * c + 1)
                    project_v(c, 1)
                if c == 0:
                    pe.wait_ge(wl_done, 4 * h + 2)
                wait(pe, k_sil, u)
                project(par, K, c, bank_k, k_done)
                if c == 0:
                    pe.wait_ge(wl_done, 4 * h + 3)
                wait(pe, g_tanh, u)
                project(par, G, c, bank_g, g_done)
                if j > 0:
                    if bc == 0:
                        pe.wait_ge(wl_done, 4 * bh + 4)
                    project_out(u - 1, bpar, 0)
                    project_out(u - 1, bpar, 1)
                pe.wait_ge(q_sil, u + 1)
                pe.wait_ge(k_sil, u + 1)
                wait(pe, s_masked, u)
                for t in range(TPC):
                    mm = pe.matmul(bank_s[:, col(t)], kt[:, col(t)], qt[:, col(t)], start=True, stop=True)
                mm.then_inc(s_done, 1)
                if j > 0:
                    project_out(u - 1, bpar, 2)
                    project_out(u - 1, bpar, 3)

            mix(0)
            pe.wait_ge(mix_lo, KH)
            unit(0, 0)
            for c in range(1, NC):
                mix(c)
            pe.wait_ge(mix_lo, 2 * KH)
            unit(0, 1, mixing=True)
            with pe.Fori(0, HEADS // 2 - 1) as i:
                for j in range(2, 10):
                    unit(i, j)
            def sum_squares(c):
                pe.wait_ge(sq_added, LAST + c + 1)
                wait(pe, ms_done, c)
                pe.matmul(bank_v[:, :], ones[:, :], sq_acc[:, ck(c)], start=True, stop=True
                          ).then_inc(ss_done, 1)

            pe.wait_ge(ones_set, 1)
            for j in range(2, 8):
                unit(HEADS // 2 - 1, j)
                if j >= 5:
                    sum_squares(j - 5)
            def transpose_a(g):
                pe.wait_ge(ld_ag[g % 4], 16 * (g // 4) + 16)
                wait(pe, at_copied, 2 * g)
                for m in range(2):
                    for k in range(KH):
                        mm = pe.transpose(banks[m][:, col(k)], ag[g % 4][:, col(KH * m + k)], ident[:, :])
                mm.then_inc(at_done, 1)

            pe.wait_ge(q_sil, UNITS)
            pe.wait_ge(k_sil, UNITS)
            pe.wait_ge(ld_late, 48)
            transpose_a(0)
            attend(UNITS - 1, 4 * (HEADS // 2), 1, NC - 1)
            pe.wait_ge(s_masked, UNITS)
            pe.wait_ge(g_tanh, UNITS)
            for g in range(NG):
                if g == 1:
                    sum_squares(NC - 1)
                if g == 3:
                    for n in range(4):
                        project_out(UNITS - 1, 1, n)
                if g + 1 < NG:
                    transpose_a(g + 1)
                pe.wait_ge(at_copied, 2 * g + 2)
                pe.wait_ge(x1_done, g // GPC + 1)
                if g >= 2:
                    pe.wait_ge(rank_masked, g - 1)
                for m in range(2):
                    for k in range(KH):
                        mm = pe.matmul(bank_rank[g % 2][:, col(m, GT)], agt[:, g % 2, col(KH * m + k)],
                                       acc[:, k, col(g, GT)], start=(k == 0), stop=(k == KH - 1))
                mm.then_inc(rank_done, 1)

            def transpose_la(u, slot, chunk_loads):
                pe.wait_ge(ld_lw[slot], 16 * GPC * chunk_loads)
                wait(pe, lal_done, u)
                for g in range(GPC):
                    mm = pe.transpose(bank_v[:, col(g)], lraw[:, slot, g, col(2)], ident[:, :])
                mm.then_inc(la_done, 1)

            def up_or_gate(u, j, part, c, dst, done):
                par, slot = j // 4 % 2, j % 2
                for k in range(KH):
                    at = slice(FW_AT[part] + k * P, FW_AT[part] + (k + 1) * P)
                    three(pe, dst[:, :], fw_hi[par][:, at], fw_lo[par][:, at],
                          hx_hi[:, k, ck(c)], hx_lo[:, k, ck(c)], k == 0, False)
                if part == 0:
                    pe.wait_ge(lbl_done, u + 1)
                for g in range(GPC):
                    at = col(GPC * c + g, GT)
                    mm = three(pe, dst[:, col(g, GT)], lb_hi[:, slot, g, col(part)],
                               lb_lo[:, slot, g, col(part)], rk_hi[:, part, at], rk_lo[:, part, at],
                               False, g == GPC - 1)
                mm.then_inc(done, 1)

            def down_ranks(u, j):
                pe.wait_ge(fal_done, u + 1)
                pe.wait_ge(lal_done, u + 1)
                wait(pe, td_acc, u)
                for g in range(GPC):
                    mm = three(pe, bank_g[:, col(g, GT)], la_hi[:, j % 2, col(g)], la_lo[:, j % 2, col(g)],
                               fa_hi[:, col(g, GT)], fa_lo[:, col(g, GT)], True, True)
                mm.then_inc(td_done, 1)

            def funit(i, j, front=True):
                u, c, par, f = 8 * i + j, j % 4, j // 4 % 2, 2 * i + j // 4
                bpar, bf = (j - 1) // 4 % 2, 2 * i + (j - 1) // 4

                def downs():
                    for n in range(KH):
                        g = KH * (u - 1) + n
                        if n == 0 and (j - 1) % 4 == 0:
                            pe.wait_ge(fl_done, FP * bf + FP)
                        if not isinstance(g, int) or g > 3:
                            pe.wait_ge(f_acc, g - 3)
                        at = slice(FW_AT[2] + n * P, FW_AT[2] + (n + 1) * P)
                        three(pe, bank_f[n][:, :], fw_hi[bpar][:, at], fw_lo[bpar][:, at],
                              fa_hi[:, :], fa_lo[:, :], True, True).then_inc(fo_done, 1)

                if front:
                    if isinstance(i, int) and i == 0:
                        pe.wait_ge(x1_lo, c + 1)
                    if isinstance(i, int) and i == 0 and j < NC:
                        pe.wait_ge(rk_lo_done, c + 1)
                    if c == 0:
                        pe.wait_ge(fl_done, FP * f + 1)
                    wait(pe, fg_sil, u)
                    up_or_gate(u, j, 0, c, bank_q, fg_done)
                if j > 0:
                    down_ranks(u - 1, j - 1)
                    downs()
                if front:
                    if not (isinstance(i, int) and u == FUNITS - 1):
                        transpose_la(u + 1, (j + 1) % 2, 4 * i + (j + 1) // 2 + 1)
                    if c == 0:
                        pe.wait_ge(fl_done, FP * f + 2)
                    wait(pe, fact_done, u)
                    up_or_gate(u, j, 1, c, bank_k, fu_done)

            pe.wait_ge(ms_done, NC)
            transpose_la(0, 0, 1)
            funit(0, 0)
            pe.wait_ge(rank_masked, NG)
            funit(0, 1)
            pe.wait_ge(x1_lo, NC)
            pe.wait_ge(rk_lo_done, NC)
            with pe.Fori(0, FC // 2 - 1) as i:
                for j in range(2, 10):
                    funit(i, j)

            def bdown(c):
                pe.wait_ge(td_masked, c + 1)
                pe.wait_ge(ld_bd[c % 3], 16 * GPC * (c // 3 + 1))
                for o in range(KH):
                    n = KH * c + o
                    if n == 2:
                        pe.wait_ge(fact_done, FUNITS)
                    if n >= 3:
                        pe.wait_ge(y_done, n - 2)
                    for g in range(GPC):
                        mm = pe.matmul(bank_bd[n % 3][:, col(g, GT)], bdg[c % 3][:, g, col(o)],
                                       td[:, col(GPC * c + g, GT)], start=True, stop=True)
                    mm.then_inc(bd_done, 1)

            for j in range(2, 12):
                funit(FC // 2 - 1, j)
            pe.wait_ge(lal_done, FUNITS)
            pe.wait_ge(fg_sil, FUNITS)
            bdown(0)
            funit(FC // 2 - 1, 12, front=False)
            bdown(1)
            bdown(2)

            def linear(c):
                if c == 0:
                    pe.wait_ge(yl0_done, KH)
                else:
                    pe.wait_ge(yl_done, KH * c)
                for o in range(KH):
                    n = KH * c + o
                    if n >= 4:
                        pe.wait_ge(res_act, n - 3)
                    for k in range(KH):
                        pe.matmul(banks[4 + n % 4][:, :], sgn[:, k, col(o)], y_hi[:, c % 2, k, :],
                                  start=(k == 0), stop=False)
                        mm = pe.matmul(banks[4 + n % 4][:, :], sgn[:, k, col(o)], y_lo[:, c % 2, k, :],
                                       start=False, stop=(k == KH - 1))
                    mm.then_inc(lin_done, 1)

            bdown(NC - 1)
            pe.wait_ge(f_acc, KH * FUNITS)
            pe.wait_ge(sgn_done, KH)
            for c in range(NC):
                linear(c)

        @block.scalar
        def _(act):
            def head_hi(n, p, par):
                act.wait_ge(ld_w[p], 16 * n + 16)
                act.activation(w_hi[par][:, p, :], raw[:, p, :], ACT.Copy).then_inc(wh_done, 1)

            def v_hi_half(m, half):
                if half == 0:
                    act.wait_ge(ld_v, 16 * m + 16)
                at = slice(2 * half, 2 * half + 2)
                act.activation(v_hi[:, at, :], raw_v[:, at, :], ACT.Copy).then_inc(vh_done, 1)

            def mix_his(c, ks=range(KH)):
                for k in ks:
                    act.wait_ge(mix_done, KH * c + k + 1)
                    act.activation(hx_hi[:, k, ck(c)], bank_mix(KH * c + k)[:, :], ACT.Copy
                                   ).then_inc(mix_hi, 1)

            def silu_v(u_v, c, half):
                act.wait_ge(v_done, 2 * u_v + half + 1)
                act.activation(vt[:, c * TPC + 2 * half:c * TPC + 2 * half + 2, :],
                               bank_v[:, :].rearrange("p (t n) -> p t n", t=2), ACT.Silu).then_inc(v_sil, 1)

            def square(u):
                act.wait_ge(o_done, u + 1)
                wait(act, sq_added, u)
                act.activation(sq[:, :], bank_o[:, :], ACT.Square).then_inc(sq_done, 1)

            def unit(i, j, ahead=True, extra=None):
                u, c, par, h, m = 8 * i + j, j % 4, j // 4 % 2, 2 * i + j // 4, i + j // 8
                if par == 0:
                    silu_v(4 * m + c, c, 0)
                act.wait_ge(q_done, u + 1)
                act.activation(qt[:, :], bank_q[:, :], ACT.Silu).then_inc(q_sil, 1)
                if j > 0:
                    square(u - 1)
                if ahead:
                    head_hi(h + 1, c, 1 - par)
                    if par == 1 and c < 2:
                        v_hi_half(m + 1, c)
                if extra:
                    extra()
                if par == 0:
                    silu_v(4 * m + c, c, 1)
                act.wait_ge(k_done, u + 1)
                act.activation(kt[:, :], bank_k[:, :], ACT.Silu).then_inc(k_sil, 1)
                act.wait_ge(g_done, u + 1)
                wait(act, t1_done, u)
                act.activation(tg[:, :], bank_g[:, :], ACT.Tanh, scale=0.5).then_inc(g_tanh, 1)

            mix_his(0, (0, 1))
            v_hi_half(0, 0)
            mix_his(0, (2,))
            v_hi_half(0, 1)
            mix_his(0, (3,))
            for p in range(4):
                head_hi(0, p, 0)
            unit(0, 0)
            for c in range(1, NC):
                mix_his(c)
            unit(0, 1)
            with act.Fori(0, HEADS // 2 - 1) as i:
                for j in range(2, 10):
                    unit(i, j)
            def root(c):
                act.wait_ge(rec_done, c + 1)
                act.activation(sq_acc[:, ck(c)], sq_acc[:, ck(c)], ACT.Sqrt).then_inc(rstd_done, 1)

            def x1_his(c):
                act.wait_ge(x1_done, c + 1)
                act.activation(hx_hi[:, :, ck(c)], acc[:, :, ck(c)], ACT.Copy).then_inc(x1_hi, 1)

            def copy_at(g):
                act.wait_ge(at_done, g + 1)
                if g >= 2:
                    act.wait_ge(rank_done, g - 1)
                for m in range(2):
                    act.activation(agt[:, g % 2, col(m, HID)], banks[m][:, :], ACT.Copy
                                   ).then_inc(at_copied, 1)

            def between():
                root(1)
                x1_his(0)

            for j in range(2, 8):
                unit(HEADS // 2 - 1, j, ahead=j < 4, extra={6: lambda: root(0), 7: between}.get(j))
            copy_at(0)
            square(UNITS - 1)
            copy_at(1)
            root(2)
            x1_his(1)
            copy_at(2)
            root(3)
            copy_at(3)
            copy_at(4)
            x1_his(2)
            copy_at(5)
            copy_at(6)
            x1_his(3)
            copy_at(7)

            def ffn_hi(f, p, par):
                act.wait_ge(ld_f[p], 16 * f + 16)
                at = slice(FW_AT[p], FW_AT[p + 1])
                act.activation(fw_hi[par][:, at], fraw[:, at], ACT.Copy).then_inc(fh_done, 1)

            def ranks_hi(c):
                act.wait_ge(rank_masked, GPC * (c + 1))
                act.activation(rk_hi[:, :, ck(c)], rk[:, :, ck(c)], ACT.Copy).then_inc(rk_hi_done, 1)

            def lora_hi(u, slot, slot_loads):
                act.wait_ge(ld_lw[slot], 16 * GPC * slot_loads)
                act.activation(lb_hi[:, slot, :, :], lraw[:, slot, :, 0:2 * P], ACT.Copy).then_inc(lbh_done, 1)
                act.wait_ge(la_done, u + 1)
                act.activation(la_hi[:, slot, :], bank_v[:, 0:GPC * P], ACT.Copy).then_inc(lah_done, 1)

            def funit(i, j, ahead=True):
                u, c, par, f = 8 * i + j, j % 4, j // 4 % 2, 2 * i + j // 4
                act.wait_ge(fg_done, u + 1)
                wait(act, fact_done, u)
                act.activation(sg, bank_q[:, :], ACT.Silu).then_inc(fg_sil, 1)
                if ahead and c < FP:
                    ffn_hi(f + 1, c, 1 - par)
                if isinstance(u, int) and u < 2:
                    for later in range(u + 1, 2 * u + 2):
                        ranks_hi(later)
                if not (isinstance(i, int) and u == FUNITS - 1):
                    lora_hi(u + 1, (j + 1) % 2, 4 * i + (j + 1) // 2 + 1)
                act.wait_ge(fact_done, u + 1)
                act.activation(fa_hi[:, :], ft, ACT.Copy).then_inc(fah_done, 1)

            act.wait_ge(x1_done, NC)
            act.wait_ge(at_done, NG)
            ranks_hi(0)
            ffn_hi(0, 0, 0)
            lora_hi(0, 0, 1)
            ffn_hi(0, 1, 0)
            ffn_hi(0, 2, 0)
            funit(0, 0)
            funit(0, 1)
            with act.Fori(0, FC // 2 - 1) as i:
                for j in range(2, 10):
                    funit(i, j)
            for j in range(2, 12):
                funit(FC // 2 - 1, j, ahead=j < 8)
                if j == 9:
                    act.wait_ge(ld_ln, 16 * KH)
                    for o in range(KH):
                        act.activation(lin_rows[o], lin_rows[o], ACT.Abs, scale=1.0 / HID,
                                       accum_out=alpha[:, o:o + 1]).then_inc(alpha_done, 1)
                if j == 11:
                    act.wait_ge(ld_lt, 16)
                    for k in range(KH):
                        act.activation(sgn[:, k, :], lin_tt[:, k, :], ACT.Sign).then_inc(sgn_done, 1)
            act.wait_ge(fu_done, FUNITS)

            def y_his(c):
                for o in range(KH):
                    n = KH * c + o
                    act.wait_ge(y_done, n + 1)
                    if c >= 2 and o == 0:
                        act.wait_ge(lin_done, KH * (c - 1))
                    act.activation(y_hi[:, c % 2, o, :], acc[:, o, ck(c)], ACT.Copy).then_inc(yh_done, 1)

            y_his(0)
            for c in range(NC):
                if c + 1 < NC:
                    y_his(c + 1)
                if c == 0:
                    act.wait_ge(alpha_done, KH)
                for o in range(KH):
                    n = KH * c + o
                    act.wait_ge(lin_done, n + 1)
                    if n >= 4:
                        act.wait_ge(stored[n % 4], 16 * (n // 4))
                    act.activation(res[:, n % 4, :], banks[4 + n % 4][:, :], ACT.Identity,
                                   scale=alpha[:, o:o + 1], bias=bias_sb[:, o:o + 1]).then_inc(res_act, 1)

        @block.vector
        def _(dve):
            dve.wait_ge(ld_small, 32)
            dve.tensor_scalar(gidx[:, :], cidx[:, :], float(SEQ), const[:, 0:1], ALU.mult, ALU.add
                              ).then_inc(idx_done, 1)
            dve.memset(mixw[:, :, :], 0.0).then_inc(mixw_zero, 1)

            def head_lo(n, p, par):
                dve.wait_ge(wh_done, 4 * n + p + 1)
                dve.tensor_tensor(w_lo[par][:, p, :], raw[:, p, :], w_hi[par][:, p, :].bitcast(F32),
                                  ALU.subtract).then_inc(wl_done, 1)

            def v_lo_half(m, half):
                dve.wait_ge(vh_done, 2 * m + half + 1)
                at = slice(2 * half, 2 * half + 2)
                dve.tensor_tensor(v_lo[:, at, :], raw_v[:, at, :], v_hi[:, at, :].bitcast(F32),
                                  ALU.subtract).then_inc(vl_done, 1)

            def mixing_weights(c):
                ts = slice(c * TPC, (c + 1) * TPC)
                dve.wait_ge(ld_gath[c], 16 * TPC)
                for b in range(4):
                    rows = slice(SEQ * b, SEQ * (b + 1))
                    dve.tensor_copy(mixw[rows, ts, rows], gath[rows, ts, :]).then_inc(mixw_done, 1)

            def mix_los(c, ks=range(KH)):
                for k in ks:
                    dve.wait_ge(mix_hi, KH * c + k + 1)
                    dve.tensor_tensor(hx_lo[:, k, ck(c)], bank_mix(KH * c + k)[:, :],
                                      hx_hi[:, k, ck(c)].bitcast(F32), ALU.subtract).then_inc(mix_lo, 1)

            dve.wait_ge(mixw_zero, 1)
            mixing_weights(0)
            mix_los(0, (0, 1))
            v_lo_half(0, 0)
            mix_los(0, (2,))
            v_lo_half(0, 1)
            mix_los(0, (3,))
            for p in range(4):
                head_lo(0, p, 0)
            for c in range(1, NC):
                mixing_weights(c)

            def mask_s(u, par):
                dve.wait_ge(s_done, u + 1)
                dve.tensor_tensor(sm[:, :].rearrange("p (t n) -> p t n", t=TPC),
                                  bank_s[:, :].rearrange("p (t n) -> p t n", t=TPC),
                                  mb[:, par, 0:P].unsqueeze(1).to_broadcast([P, TPC, P]),
                                  ALU.mult).then_inc(s_masked, 1)

            def gate_o(u, par, c):
                dve.wait_ge(g_tanh, u + 1)
                dve.wait_ge(sq_done, u + 1)
                dve.scalar_tensor_tensor(out=t1[:, :], in0=tg[:, :], scalar=1.0, in1=bank_o[:, :],
                                         op0=ALU.add, op1=ALU.mult).then_inc(t1_done, 1)
                dve.wait_ge(t1_done, u + 1)
                dve.tensor_scalar(go_hi[:, :], t1[:, :], mb[:, par, P:P + 1], None, ALU.mult
                                  ).then_inc(goh_done, 1)
                dve.wait_ge(goh_done, u + 1)
                dve.scalar_tensor_tensor(out=go_lo[:, :], in0=t1[:, :], scalar=mb[:, par, P:P + 1],
                                         in1=go_hi[:, :].bitcast(F32), op0=ALU.mult, op1=ALU.subtract
                                         ).then_inc(go_done, 1)
                dve.tensor_tensor(sq_acc[:, ck(c)], sq_acc[:, ck(c)], sq[:, :], ALU.add
                                  ).then_inc(sq_added, 1)

            def add_out(u, c, n):
                dve.wait_ge(out_done, 4 * u + n + 1)
                dve.tensor_tensor(acc[:, n, ck(c)], acc[:, n, ck(c)], bank_out[n % 2][:, :], ALU.add
                                  ).then_inc(out_acc, 1)

            def unit(i, j, ahead=True, extra=None):
                u, c, par, h, m = 8 * i + j, j % 4, j // 4 % 2, 2 * i + j // 4, i + j // 8
                bc, bpar = (j - 1) % 4, (j - 1) // 4 % 2
                if j > 0:
                    gate_o(u - 1, bpar, bc)
                if extra:
                    extra()
                if ahead:
                    head_lo(h + 1, c, 1 - par)
                    if par == 1 and c < 2:
                        v_lo_half(m + 1, c)
                if j > 0:
                    add_out(u - 1, bc, 0)
                    add_out(u - 1, bc, 1)
                if c == 0:
                    dve.wait_ge(ld_m[par], 16 * (i + j // 8) + 16)
                mask_s(u, par)
                if j > 0:
                    add_out(u - 1, bc, 2)
                    add_out(u - 1, bc, 3)

            unit(0, 0)
            for c in range(1, NC):
                mix_los(c)
            dve.wait_ge(acc_zero, 2)
            unit(0, 1)
            dve.wait_ge(acc_zero, 1 + NC)

            dve.wait_ge(ld_late, 48)
            dve.tensor_scalar(aidx[:, :], ridx[:, :], float(RANK), const[:, 1:2], ALU.mult, ALU.add
                              ).then_inc(ridx_done, 1)
            dve.wait_ge(ridx_done, 1)
            for par in range(2):
                dve.tensor_scalar(fidx[:, par, :], aidx[:, :], float(par * CONDS * RANK), None, ALU.add
                                  ).then_inc(ridx_done, 1)
            with dve.Fori(0, HEADS // 2 - 1) as i:
                for j in range(2, 10):
                    unit(i, j)
            def mean(c):
                at = sq_acc[:, ck(c)]
                dve.wait_ge(ss_done, c + 1)
                dve.tensor_scalar(at, bank_v[:, :], 4.0 / HD, EPS, ALU.mult, ALU.add).then_inc(ms_done, 1)
                dve.wait_ge(ms_done, c + 1)
                dve.reciprocal(at, at).then_inc(rec_done, 1)

            def scale_o(c):
                at = acc[:, :, ck(c)]
                dve.wait_ge(rstd_done, c + 1)
                dve.tensor_tensor(at, at, sq_acc[:, ck(c)].unsqueeze(1).to_broadcast([P, KH, NT]),
                                  ALU.mult).then_inc(nrm_done, 1)

            def add_x(c):
                at = acc[:, :, ck(c)]
                dve.wait_ge(nrm_done, c + 1)
                dve.wait_ge(ld_xt[c], 16)
                dve.tensor_tensor(at, at, x_c[c], ALU.add).then_inc(x1_done, 1)

            def mask_ranks(g):
                dve.wait_ge(rank_done, g + 1)
                dve.tensor_tensor(rk[:, :, col(g, GT)].rearrange("p m (b s) -> p m b s", s=SEQ),
                                  bank_rank[g % 2][:, :].rearrange("p (m b s) -> p m b s", m=2, s=SEQ),
                                  const[:, 2:2 + GB].unsqueeze(1).unsqueeze(3).to_broadcast([P, 2, GB, SEQ]),
                                  ALU.mult).then_inc(rank_masked, 1)

            for j in range(2, 8):
                unit(HEADS // 2 - 1, j, ahead=j < 4,
                     extra={6: lambda: scale_o(0), 7: lambda: scale_o(1)}.get(j))
                if j in (6, 7):
                    add_x(j - 6)
                if j in (5, 6):
                    mean(j - 5)
            gate_o(UNITS - 1, 1, NC - 1)
            mean(2)
            mask_ranks(0)
            mean(3)
            mask_ranks(1)
            for n in range(4):
                add_out(UNITS - 1, NC - 1, n)
            mask_ranks(2)
            scale_o(2)
            add_x(2)
            mask_ranks(3)
            scale_o(3)
            add_x(3)
            mask_ranks(4)
            mask_ranks(5)

            def ranks_lo(c):
                dve.wait_ge(rk_hi_done, c + 1)
                dve.tensor_tensor(rk_lo[:, :, ck(c)], rk[:, :, ck(c)], rk_hi[:, :, ck(c)].bitcast(F32),
                                  ALU.subtract).then_inc(rk_lo_done, 1)

            def lora_lo(u, slot):
                dve.wait_ge(lbh_done, u + 1)
                dve.tensor_tensor(lb_lo[:, slot, :, :], lraw[:, slot, :, 0:2 * P],
                                  lb_hi[:, slot, :, :].bitcast(F32), ALU.subtract).then_inc(lbl_done, 1)
                dve.wait_ge(lah_done, u + 1)
                dve.tensor_tensor(la_lo[:, slot, :], bank_v[:, 0:GPC * P],
                                  la_hi[:, slot, :].bitcast(F32), ALU.subtract).then_inc(lal_done, 1)

            def ffn_lo(f, p, par):
                dve.wait_ge(fh_done, FP * f + p + 1)
                at = slice(FW_AT[p], FW_AT[p + 1])
                dve.tensor_tensor(fw_lo[par][:, at], fraw[:, at], fw_hi[par][:, at].bitcast(F32),
                                  ALU.subtract).then_inc(fl_done, 1)

            def add_down(u, c, n):
                dve.wait_ge(fo_done, KH * u + n + 1)
                dve.tensor_tensor(acc[:, n, ck(c)], acc[:, n, ck(c)], bank_f[n][:, :], ALU.add
                                  ).then_inc(f_acc, 1)

            def add_td(u, c):
                dve.wait_ge(td_done, u + 1)
                dve.tensor_tensor(td[:, ck(c)], td[:, ck(c)], bank_g[:, :], ALU.add).then_inc(td_acc, 1)

            def funit(i, j, ahead=True):
                u, c, par, f = 8 * i + j, j % 4, j // 4 % 2, 2 * i + j // 4
                bc = (j - 1) % 4
                if j > 0:
                    add_td(u - 1, bc)
                    for n in range(KH):
                        add_down(u - 1, bc, n)
                if ahead and c < FP:
                    ffn_lo(f + 1, c, 1 - par)
                if isinstance(u, int) and u < 2:
                    for later in range(u + 1, 2 * u + 2):
                        ranks_lo(later)
                if not (isinstance(i, int) and u == FUNITS - 1):
                    lora_lo(u + 1, (j + 1) % 2)
                dve.wait_ge(fu_done, u + 1)
                dve.wait_ge(fg_sil, u + 1)
                dve.tensor_tensor(ft, sg, bank_k[:, :], ALU.mult).then_inc(fact_done, 1)
                dve.wait_ge(fah_done, u + 1)
                dve.tensor_tensor(fa_lo[:, :], ft, fa_hi[:, :].bitcast(F32), ALU.subtract
                                  ).then_inc(fal_done, 1)

            ranks_lo(0)
            ffn_lo(0, 0, 0)
            lora_lo(0, 0)
            mask_ranks(6)
            mask_ranks(7)
            ffn_lo(0, 1, 0)
            ffn_lo(0, 2, 0)
            funit(0, 0)
            dve.wait_ge(facc_zero, 1 + NC)
            funit(0, 1)
            with dve.Fori(0, FC // 2 - 1) as i:
                for j in range(2, 10):
                    funit(i, j)

            def mask_td(c):
                dve.wait_ge(td_acc, FUNITS - NC + c + 1)
                at = td[:, ck(c)].rearrange("p (g b s) -> p g b s", g=GPC, s=SEQ)
                half = const[:, 2:2 + GB].unsqueeze(1).unsqueeze(3).to_broadcast([P, GPC, GB, SEQ])
                dve.tensor_tensor(at, at, half, ALU.mult).then_inc(td_masked, 1)

            def add_bdown(c):
                for o in range(KH):
                    n = KH * c + o
                    dve.wait_ge(bd_done, n + 1)
                    dve.tensor_tensor(acc[:, o, ck(c)], acc[:, o, ck(c)], bank_bd[n % 3][:, :], ALU.add
                                      ).then_inc(y_done, 1)

            for j in range(2, 12):
                funit(FC // 2 - 1, j, ahead=j < 8)
                if j == 11:
                    add_bdown(0)
                if j >= 9:
                    mask_td(j - 9)
            add_td(FUNITS - 1, NC - 1)
            mask_td(NC - 1)
            add_bdown(1)
            for n in range(KH):
                add_down(FUNITS - 1, NC - 1, n)

            def y_los(c):
                for o in range(KH):
                    n = KH * c + o
                    dve.wait_ge(yh_done, n + 1)
                    dve.tensor_tensor(y_lo[:, c % 2, o, :], acc[:, o, ck(c)],
                                      y_hi[:, c % 2, o, :].bitcast(F32), ALU.subtract).then_inc(yl_done, 1)

            add_bdown(2)
            add_bdown(3)
            for c in range(NC):
                if c + 1 < NC:
                    y_los(c + 1)
                for o in range(KH):
                    n = KH * c + o
                    r = res[:, n % 4, :]
                    dve.wait_ge(res_act, n + 1)
                    dve.tensor_tensor(r, r, hx_hi[:, o, ck(c)].bitcast(F32), ALU.add).then_inc(res_a, 1)
                    dve.wait_ge(res_a, n + 1)
                    dve.tensor_tensor(r, r, hx_lo[:, o, ck(c)].bitcast(F32), ALU.add).then_inc(res_done, 1)


def decay_masks():
    layer, layers = 1, 32
    base = np.float32(1.0 / 2.0 ** (8.0 / HEADS))
    factor = np.float32(1.0 - layer / (layers - 1 + 1e-05) + 1e-05)
    slope = base ** (np.arange(HEADS, dtype=np.float32) + 1) * factor
    diff = np.arange(SEQ)[None, :] - np.arange(SEQ)[:, None]
    one = np.where(diff >= 0, np.exp(-slope[:, None, None] * np.maximum(diff, 0)), 0.0) * 0.5
    full = np.zeros((HEADS, P, P), np.float32)
    for b in range(P // SEQ):
        full[:, b * SEQ:(b + 1) * SEQ, b * SEQ:(b + 1) * SEQ] = one
    return full


def kernel(**inputs):
    import concourse.bacc as bacc
    from concourse.bass_utils import run_bass_kernel_spmd

    x = np.asarray(inputs["x"])
    cond = np.asarray(inputs["itok_B_0_15"]).astype(np.int32)
    lora = np.asarray(inputs["itok_B_2_6"]).astype(np.int32)

    def chunked(w):
        return np.asarray(w).reshape(-1, KH, P).transpose(2, 1, 0)

    qkv = np.asarray(inputs["L0_attn_qkv_w"]).reshape(HEADS, 3, D, KH, P)
    by_head = qkv.transpose(0, 1, 4, 3, 2)
    gate = np.asarray(inputs["L0_attn_gate_w"]).reshape(HEADS, D, KH, P).transpose(0, 3, 2, 1)
    outw = np.asarray(inputs["L0_attn_out_w"]).reshape(HID, HEADS, D).transpose(1, 2, 0)
    head_w = np.stack([by_head[:, 0].reshape(HEADS, P, HID), by_head[:, 1].reshape(HEADS, P, HID),
                       gate.reshape(HEADS, P, HID), outw], 1)
    v_w = by_head[:, 2].reshape(HEADS // 2, 2, P, KH, D).transpose(0, 2, 3, 1, 4).reshape(
        HEADS // 2, P, KH, 2 * D)
    norm = np.asarray(inputs["L0_attn_norm_w"]).reshape(HEADS, D, 1)
    misc = np.concatenate([decay_masks(), norm], 2)

    def padded(w, axis):
        shape = list(w.shape)
        shape[axis] = FC * P - F
        return np.concatenate([w, np.zeros(shape, w.dtype)], axis)

    def hidden(w):
        return padded(np.asarray(w), 0).reshape(FC, P, KH, P).transpose(0, 3, 2, 1).reshape(FC, P, HID)

    down_w = padded(np.asarray(inputs["L0_cond2_W_down"]), 1).reshape(HID, FC, P).transpose(1, 2, 0)
    ffn_w = np.concatenate([hidden(inputs["L0_cond2_W_gate"]), hidden(inputs["L0_cond2_W_up"]),
                            down_w], 2)

    def ranks(w):
        w = padded(np.asarray(w)[0], 1).transpose(0, 2, 1).reshape(CONDS * RANK, FC, P)
        return w.transpose(1, 0, 2).reshape(FC * CONDS * RANK, P)

    adown = padded(np.asarray(inputs["L0_cond2_A_down"])[0], 2).reshape(CONDS * RANK, FC, P)
    b_w = np.concatenate([ranks(inputs["L0_cond2_B_gate"]), ranks(inputs["L0_cond2_B_up"]),
                          adown.transpose(1, 0, 2).reshape(FC * CONDS * RANK, P)], 1)
    a_w = np.concatenate([np.asarray(inputs[n])[0].reshape(CONDS * RANK, HID)
                          for n in ("L0_cond2_A_gate", "L0_cond2_A_up")], 1)
    bdown = np.asarray(inputs["L0_cond2_B_down"])[0].transpose(0, 2, 1).reshape(CONDS * RANK, HID)
    lin = np.asarray(inputs["L0_ffn_weight_real"])
    rows = np.arange(P)
    consts = np.stack([rows % SEQ, rows % RANK]
                      + [0.5 * (rows // RANK == j) for j in range(GB)], 1).astype(np.float32)
    arrays = dict(
        x_tok=x.reshape(TILES, P, HID).transpose(1, 0, 2),
        x_t=x.reshape(NC, NT, KH, P).transpose(3, 0, 2, 1).reshape(P, NC, KH * NT),
        cond_idx=np.repeat(cond.reshape(TILES, 4).T, SEQ, 0),
        rank_idx=np.repeat(lora.reshape(NG, GB).T, RANK, 0),
        consts=consts, eye=np.eye(P, dtype=np.float32),
        cond_w=np.asarray(inputs["L0_cond_weights"]).reshape(CONDS * SEQ, SEQ),
        head_w=head_w, v_w=v_w, misc=misc, a_w=a_w, ffn_w=ffn_w, b_w=b_w, bdown_w=bdown,
        lin_n=lin.reshape(KH, P, HID), lin_t=chunked(lin),
        bias=np.asarray(inputs["L0_ffn_bias"]).reshape(KH, P).T,
    )
    arrays = {n: np.ascontiguousarray(a) for n, a in arrays.items()}
    nc = bacc.Bacc("TRN2", target_bir_lowering=False, num_devices=1)
    args = {n: nc.dram_tensor(n + "_dram", a.shape, mybir.dt.from_np(a.dtype), kind="ExternalInput").ap()
            for n, a in arrays.items()}
    out = nc.dram_tensor("out_dram", (KH, P, TOK), F32, kind="ExternalOutput").ap()
    build(nc, *args.values(), out)
    r = run_bass_kernel_spmd(nc, [{n + "_dram": a for n, a in arrays.items()}], core_ids=[0])
    got = np.asarray(r.results[0]["out_dram"])
    return got.reshape(HID, TOK).T.reshape(BATCH, SEQ, HID)
```
